# Optimizing a Trainium2 kernel written in Bass

```python
import numpy as np
import jax
import jax.numpy as jnp

def _softmax(x, axis=-1):
    return jax.nn.softmax(x, axis=axis)

def _gelu(x):
    return jax.nn.gelu(x, approximate=True)

def _silu(x):
    return jax.nn.silu(x)

def _sigmoid(x):
    return jax.nn.sigmoid(x)

def _layernorm(x, axis=-1, eps=1e-05):
    m = jnp.mean(x, axis=axis, keepdims=True)
    v = jnp.var(x, axis=axis, keepdims=True)
    return (x - m) / jnp.sqrt(v + eps)

def _scatter_add(tgt, idx, src, axis=0):
    return tgt.at[idx].add(src)

def _segment_sum(src, seg, n):
    return jax.ops.segment_sum(src, seg, n)
kernel_name = 'mk_conv_attn_hybrid_d2_conv_nchw512_r4_bd6749'

def setup_inputs(seed: int=0):
    np.random.seed(seed)
    _w = jnp.asarray

    def _rec_inputs():
        import jax
        import jax.numpy as jnp
        _gk = jax.random.key(seed)
        x = -0.0003957 + 1 * jax.random.normal(jax.random.fold_in(_gk, 1), (8, 128, 56, 56), jnp.float32)
        return x
    x = _rec_inputs()

    def _L0_conv_setup():
        import jax, jax.numpy as jnp
        import numpy as np
        KSZ = 7
        HEADS = 16
        DIM = 128
        key = jax.random.key(seed)
        k0, k1, k2, k3 = jax.random.split(key, 4)
        B, C, H, W = (8, DIM, 56, 56)
        x = jax.random.normal(k0, (B, C, H, W), jnp.float32)
        qkv_w = jax.random.normal(k1, (3 * C, C), jnp.float32) * 0.02
        rpb = jax.random.normal(k2, (HEADS, 2 * KSZ - 1, 2 * KSZ - 1), jnp.float32) * 0.02
        proj_w = jax.random.normal(k3, (C, C), jnp.float32) * 0.02
        proj_b = jnp.zeros((C,), jnp.float32)
        return {'x': x, 'qkv_w': qkv_w, 'rpb': rpb, 'proj_w': proj_w, 'proj_b': proj_b}
    _L0_conv_all = _L0_conv_setup()
    _L0_conv_in = {k: v for k, v in _L0_conv_all.items() if k in ('qkv_w', 'rpb', 'proj_w', 'proj_b')}
    del _L0_conv_all

    def _L1_attn_setup():
        import jax, jax.numpy as jnp
        import numpy as np
        EMBED_DIM = 128
        NUM_HEADS = 8
        HEAD_DIM = EMBED_DIM // NUM_HEADS

        def _split_heads(x, B, S):
            return x.reshape(B, S, NUM_HEADS, HEAD_DIM).transpose(0, 2, 1, 3)
        key = jax.random.key(seed)
        ks = jax.random.split(key, 6)
        B, S, D = (2, 1024, EMBED_DIM)
        scale = 1.0 / np.sqrt(D)
        inputs = jax.random.normal(ks[0], (B, S, D), dtype=jnp.float32)
        Wq = jax.random.normal(ks[1], (D, D), dtype=jnp.float32) * scale
        Wk = jax.random.normal(ks[2], (D, D), dtype=jnp.float32) * scale
        Wv = jax.random.normal(ks[3], (D, D), dtype=jnp.float32) * scale
        Wo = jax.random.normal(ks[4], (D, D), dtype=jnp.float32) * scale
        zeros = jnp.zeros((D,), dtype=jnp.float32)
        return {'inputs': inputs, 'Wq': Wq, 'bq': zeros, 'Wk': Wk, 'bk': zeros, 'Wv': Wv, 'bv': zeros, 'Wo': Wo, 'bo': zeros}
    _L1_attn_all = _L1_attn_setup()
    _L1_attn_in = {k: v for k, v in _L1_attn_all.items() if k in ('Wq', 'bq', 'Wk', 'bk', 'Wv', 'bv', 'Wo', 'bo')}
    del _L1_attn_all

    def _L1_ffn_setup():
        import jax, jax.numpy as jnp
        import numpy as np
        BLOCK = 16
        NF4_TABLE = jnp.array([-1.0, -0.6961928009986877, -0.5250730514526367, -0.39491748809814453, -0.28444138169288635, -0.18477343022823334, -0.09105003625154495, 0.0, 0.07958029955625534, 0.16093020141124725, 0.24611230194568634, 0.33791524171829224, 0.44070982933044434, 0.5626170039176941, 0.7229568362236023, 1.0], dtype=jnp.float32)

        def _dequant_nf4(qidx, scales):
            w = NF4_TABLE[qidx].reshape(-1, BLOCK) * scales[:, None]
            return w.reshape(qidx.shape)
        key = jax.random.key(seed)
        k1, k2, k3, k4 = jax.random.split(key, 4)
        x = jax.random.normal(k1, (4, 2048, 128), dtype=jnp.float32)
        qidx = jax.random.randint(k2, (128, 128), 0, 16, dtype=jnp.int32)
        scales = jax.random.uniform(k3, (1024,), dtype=jnp.float32)
        W = jax.random.normal(k4, (128, 128), dtype=jnp.float32) * (1.0 / np.sqrt(512.0))
        return {'x': x, 'qidx': qidx, 'scales': scales, 'W': W}
    _L1_ffn_all = _L1_ffn_setup()
    _L1_ffn_in = {k: v for k, v in _L1_ffn_all.items() if k in ('qidx', 'scales', 'W')}
    del _L1_ffn_all
    return {'x': x, 'L0_conv_qkv_w': _L0_conv_in['qkv_w'], 'L0_conv_rpb': _L0_conv_in['rpb'], 'L0_conv_proj_w': _L0_conv_in['proj_w'], 'L0_conv_proj_b': _L0_conv_in['proj_b'], 'L1_attn_Wq': _L1_attn_in['Wq'], 'L1_attn_bq': _L1_attn_in['bq'], 'L1_attn_Wk': _L1_attn_in['Wk'], 'L1_attn_bk': _L1_attn_in['bk'], 'L1_attn_Wv': _L1_attn_in['Wv'], 'L1_attn_bv': _L1_attn_in['bv'], 'L1_attn_Wo': _L1_attn_in['Wo'], 'L1_attn_bo': _L1_attn_in['bo'], 'L1_ffn_qidx': _L1_ffn_in['qidx'], 'L1_ffn_scales': _L1_ffn_in['scales'], 'L1_ffn_W': _L1_ffn_in['W']}

def reference(x, L0_conv_qkv_w, L0_conv_rpb, L0_conv_proj_w, L0_conv_proj_b, L1_attn_Wq, L1_attn_bq, L1_attn_Wk, L1_attn_bk, L1_attn_Wv, L1_attn_bv, L1_attn_Wo, L1_attn_bo, L1_ffn_qidx, L1_ffn_scales, L1_ffn_W):
    import jax
    import jax.numpy as jnp

    def _L0_conv_ref(x, qkv_w, rpb, proj_w, proj_b):
        import jax, jax.numpy as jnp
        import numpy as np
        KSZ = 7
        HEADS = 16
        DIM = 128
        B, C, H, W = x.shape
        h, d = (HEADS, C // HEADS)
        scale = d ** (-0.5)
        r = KSZ // 2
        xf = x.transpose(0, 2, 3, 1)
        qkv = (xf @ qkv_w.T).reshape(B, H, W, 3, h, d).transpose(3, 0, 4, 1, 2, 5)
        q, k, v = (qkv[0] * scale, qkv[1], qkv[2])
        si = jnp.clip(jnp.arange(H) - r, 0, H - KSZ)
        sj = jnp.clip(jnp.arange(W) - r, 0, W - KSZ)
        ii = jnp.arange(H)
        jj = jnp.arange(W)
        logits = []
        for a in range(KSZ):
            ka = jnp.take(k, si + a, axis=2)
            bias_i = rpb[:, si + a - ii + (KSZ - 1)]
            for c in range(KSZ):
                kac = jnp.take(ka, sj + c, axis=3)
                bj = sj + c - jj + (KSZ - 1)
                l = jnp.einsum('bhijd,bhijd->bhij', q, kac) + bias_i[:, :, bj][None]
                logits.append(l)
        logits = jnp.stack(logits, axis=-1)
        attn = jax.nn.softmax(logits, axis=-1)
        out = jnp.zeros_like(q)
        t = 0
        for a in range(KSZ):
            va = jnp.take(v, si + a, axis=2)
            for c in range(KSZ):
                vac = jnp.take(va, sj + c, axis=3)
                out = out + attn[..., t, None] * vac
                t += 1
        out = out.transpose(0, 2, 3, 1, 4).reshape(B, H, W, C)
        y = out @ proj_w.T + proj_b
        return y.transpose(0, 3, 1, 2)

    def _L1_attn_ref(inputs, Wq, bq, Wk, bk, Wv, bv, Wo, bo):
        import jax, jax.numpy as jnp
        import numpy as np
        EMBED_DIM = 128
        NUM_HEADS = 8
        HEAD_DIM = EMBED_DIM // NUM_HEADS

        def _split_heads(x, B, S):
            return x.reshape(B, S, NUM_HEADS, HEAD_DIM).transpose(0, 2, 1, 3)
        B, S, D = inputs.shape
        q = _split_heads(inputs @ Wq + bq, B, S)
        k = _split_heads(inputs @ Wk + bk, B, S)
        v = _split_heads(inputs @ Wv + bv, B, S)
        scale = 1.0 / jnp.sqrt(jnp.asarray(HEAD_DIM, dtype=inputs.dtype))
        scores = jnp.einsum('bhqd,bhkd->bhqk', q, k) * scale
        weights = jax.nn.softmax(scores, axis=-1)
        attn = jnp.einsum('bhqk,bhkd->bhqd', weights, v)
        attn = attn.transpose(0, 2, 1, 3).reshape(B, S, D)
        return attn @ Wo + bo

    def _L1_ffn_ref(x, qidx, scales, W):
        import jax, jax.numpy as jnp
        import numpy as np
        BLOCK = 16
        NF4_TABLE = jnp.array([-1.0, -0.6961928009986877, -0.5250730514526367, -0.39491748809814453, -0.28444138169288635, -0.18477343022823334, -0.09105003625154495, 0.0, 0.07958029955625534, 0.16093020141124725, 0.24611230194568634, 0.33791524171829224, 0.44070982933044434, 0.5626170039176941, 0.7229568362236023, 1.0], dtype=jnp.float32)

        def _dequant_nf4(qidx, scales):
            w = NF4_TABLE[qidx].reshape(-1, BLOCK) * scales[:, None]
            return w.reshape(qidx.shape)
        w_lora = _dequant_nf4(qidx, scales)
        y = jnp.einsum('bsd,od->bso', x, w_lora)
        out = jnp.einsum('bsd,od->bso', y, W)
        return out

    def _gn(v, G=32, eps=1e-05):
        B_, C_, H_, W_ = v.shape
        g = v.reshape(B_, G, C_ // G, H_, W_)
        m = jnp.mean(g, axis=(2, 3, 4), keepdims=True)
        s = jnp.var(g, axis=(2, 3, 4), keepdims=True)
        return ((g - m) / jnp.sqrt(s + eps)).reshape(v.shape)

    def _ln_c(v, eps=1e-06):
        m = jnp.mean(v, axis=1, keepdims=True)
        s = jnp.var(v, axis=1, keepdims=True)
        return (v - m) / jnp.sqrt(s + eps)

    def _ln_t(v, eps=1e-05):
        m = jnp.mean(v, axis=-1, keepdims=True)
        s = jnp.var(v, axis=-1, keepdims=True)
        return (v - m) / jnp.sqrt(s + eps)

    def _to_tokens(v):
        B_, C_, H_, W_ = v.shape
        return v.reshape(B_, C_, H_ * W_).transpose(0, 2, 1)

    def _from_tokens(t, like):
        B_, C_, H_, W_ = like.shape
        return t.transpose(0, 2, 1).reshape(B_, C_, H_, W_)
    x = x + _L0_conv_ref(_gn(x), L0_conv_qkv_w, L0_conv_rpb, L0_conv_proj_w, L0_conv_proj_b)
    t = _to_tokens(x)
    t = t + _L1_attn_ref(_ln_t(t), L1_attn_Wq, L1_attn_bq, L1_attn_Wk, L1_attn_bk, L1_attn_Wv, L1_attn_bv, L1_attn_Wo, L1_attn_bo)
    t = t + _L1_ffn_ref(_ln_t(t), L1_ffn_qidx, L1_ffn_scales, L1_ffn_W)
    x = _from_tokens(t, x)
    return x

_drawn_inputs = setup_inputs


def setup_inputs(seed=0):
    import zlib

    import numpy as np

    out = dict(_drawn_inputs(seed))
    spreads = {'L0_conv_proj_b': (0.0, 0.1),
     'L1_attn_bq': (0.0, 0.671),
     'L1_attn_bk': (0.0, 0.8),
     'L1_attn_bv': (0.0, 0.1),
     'L1_attn_bo': (0.0, 0.1)}
    factors = {'L0_conv_qkv_w': 7.764, 'L0_conv_rpb': 8.0, 'L0_conv_proj_w': 7.777}
    for name, (base, spread) in spreads.items():
        noise = np.random.default_rng([zlib.crc32(name.encode()), seed]).standard_normal(out[name].shape)
        drawn = base * np.exp(spread * noise) if base else spread * noise
        out[name] = jnp.asarray(drawn.astype(out[name].dtype))
    for name, factor in factors.items():
        out[name] = (out[name] * factor).astype(out[name].dtype)
    return out
```

```python
from contextlib import ExitStack

import numpy as np

import concourse.bass as bass
from concourse import mybir

F32 = mybir.dt.float32
BF16 = mybir.dt.bfloat16
I32 = mybir.dt.int32
ALU = mybir.AluOpType
ACT = mybir.ActivationFunctionType
AX = mybir.AxisListType

P = 128
SIDE = 56
TOK = SIDE * SIDE
BLK = 448
NBLK = TOK // BLK

KSZ = 7
NHEADS = 16
NDIM = P // NHEADS
QI, QJ = 2, 4
WI, WJ = QI + KSZ - 1, QJ + KSZ - 1
KEYS = WI * WJ
UNITS = SIDE // QJ
STRIPS = SIDE // QI
PADJ = KSZ // 2
WIDE = SIDE + 2 * PADJ
VROW = SIDE * 2
MASKED = -1.0e30
ROW_TYPES = [0, 1, 2, STRIPS - 2, STRIPS - 1]
S_BANK = [5, 5, 4]
KPAD = 96

PRIMED = 1

AHEADS = 8
ADIM = P // AHEADS
GH = 4
GROUPS = AHEADS // GH
CHUNKS = -(-TOK // P)
TOKP = CHUNKS * P
LAST = TOK - (CHUNKS - 1) * P
Q_PARTS = [0, 1, 2, 0, 1, 0]
K_PARTS = [0, 0, 0, 1, 1, 2]
ROWS = len(Q_PARTS) * ADIM
ROWSM = ROWS + 3

OWN = 27

NF4 = [-1.0, -0.6961928009986877, -0.5250730514526367, -0.39491748809814453, -0.28444138169288635,
       -0.18477343022823334, -0.09105003625154495, 0.0, 0.07958029955625534, 0.16093020141124725,
       0.24611230194568634, 0.33791524171829224, 0.44070982933044434, 0.5626170039176941,
       0.7229568362236023, 1.0]
NF4_BLOCK = 16


def shape_constants():
    c = np.zeros((P, 4 * P + GH + 3), np.float32)
    p = np.arange(P)
    c[:, 0:P] = np.eye(P)
    c[:, P:2 * P] = 1.0 / P
    c[:, 2 * P:3 * P] = (p[:, None] // 4 == p[None, :] // 4) / 4.0
    c[:, 3 * P:4 * P] = p[:, None] == 32 * (p[None, :] // 32) + ADIM
    c[:, 4 * P:4 * P + GH] = (p[:, None] % 32) // NDIM == np.arange(GH)[None, :]
    c[:, 4 * P + GH] = 1e-5
    c[:, 4 * P + GH + 1] = 1.0
    return c


def window_row(strip):
    return min(max(QI * strip - KSZ // 2, 0), SIDE - WI)


def first_key(i):
    return min(max(i - KSZ // 2, 0), SIDE - KSZ)


def hybrid_block(nc, images, x, consts, qkv_wT, rpb, proj_wT, proj_b, Wq, bq, Wk, bk, Wv, bv, Wo, bo,
                 qidx, scales, WT, out):
    vT_dram = nc.dram_tensor("vT_padded", (SIDE * WIDE, P), F32, kind="Internal").ap()

    with ExitStack() as ctx:
        def sb(name, shape, dt=F32):
            return ctx.enter_context(nc.sbuf_tensor(name, shape, dt))

        def sem(name):
            return ctx.enter_context(nc.semaphore(name))

        X = sb("X", [P, TOK])
        C = sb("C", [P, consts.shape[1]])
        ident, mean_w = C[:, 0:P], C[:, P:2 * P]
        group_w, pick_sum = C[:, 2 * P:3 * P], C[:, 3 * P:4 * P]
        head_mask = C[:, 4 * P:4 * P + GH]
        eps5 = C[:, 4 * P + GH:4 * P + GH + 1]
        W_qkv = sb("W_qkv", [P, 3 * P])
        W_proj = sb("W_proj", [P, P])
        W_q, W_k, W_v = sb("W_q", [P, P]), sb("W_k", [P, P]), sb("W_v", [P, P])
        W_o = sb("W_o", [P, GROUPS, P])
        W_ffn = sb("W_ffn", [P, P])
        bias_cols = sb("bias_cols", [P, 4])
        bv_rows = sb("bv_rows", [P, P])
        nat_bias = sb("nat_bias", [P, len(ROW_TYPES), 3, KEYS])
        KP = sb("KP", [P, GROUPS, GH, TOK], BF16)
        ones96 = sb("ones96", [P, 32])
        stats = sb("stats", [P, NBLK, 6])
        gn = sb("gn", [P, 12])
        maxes = sb("maxes", [P, 2, GH * CHUNKS])
        shift = sb("shift", [P, 2, P])
        shift_parts = sb("shift_parts", [P, 3, P], BF16)
        tail = sb("tail", [P, 2, BLK])
        normed = sb("normed", [P, BLK])
        scale_blocks = sb("scale_blocks", [P, P // NF4_BLOCK])

        arena = sb("arena", [P, 32192])

        def part(at, n, dt=F32):
            v = arena[:, at:at + n]
            return v if dt == F32 else v.bitcast(dt)

        QP = part(0, 12800, BF16).rearrange("p (g h t) -> p g h t", g=GROUPS, h=GH)
        q_parts = part(12800, 4704, BF16).rearrange("p (n t) -> p n t", n=3)
        k_parts = part(17504, 4704, BF16).rearrange("p (n t) -> p n t", n=3)
        VA = part(22208, 6400).rearrange("p (c h e) -> p c h e", c=CHUNKS, h=AHEADS)
        PB = part(28608, 3584).rearrange("p (s h t) -> p s h t", s=2, h=GH)
        XN = part(28608, TOK)
        SD, SQ = part(0, TOK), part(12800, TOK)
        q_full, q_rest = part(3200, TOK), part(6400, TOK)
        k_full, k_rest = part(9600, TOK), part(0, TOK)
        Qn = part(0, TOK)
        Kn = part(3136, SIDE * WIDE)
        VTs = part(6608, 28 * P).rearrange("p (c e) -> p c e", c=28)
        QB = part(10192, 2 * UNITS * 32).rearrange("p (s u e) -> p s u e", s=2, u=UNITS)
        KS = part(11088, 2 * WI * WIDE).rearrange("p (s n) -> p s n", s=2)
        SC = part(12080, 2 * UNITS * KEYS).rearrange("p (s u k) -> p s u k", s=2, u=UNITS)
        PT = part(14320, 2 * UNITS * P).rearrange("p (s u e) -> p s u e", s=2, u=UNITS)
        VP = part(17904, 2 * UNITS * P).rearrange("p (s u e) -> p s u e", s=2, u=UNITS)
        RS = part(21488, 2 * BLK).rearrange("p (s n) -> p s n", s=2)
        RM = part(22384, 2 * BLK).rearrange("p (s n) -> p s n", s=2)
        PVM = part(23280, BLK)
        NM = part(23728, 32).rearrange("p (s n) -> p s n", s=2)
        On = part(23760, TOK)

        W_up, codes = part(1000, P), part(1200, P, I32)

        PS = ctx.enter_context(nc.psum_tensor("PS", [P, 8, 512], F32))

        weights_in = sem("weights_in")
        paced = sem("paced")
        table_filled, table_rows_in, table_cols_in = sem("table_filled"), sem("table_rows_in"), sem("table_cols_in")
        vpad_out = sem("vpad_out")
        setup_dve, setup_pool, setup_pe = sem("setup_dve"), sem("setup_pool"), sem("setup_pe")
        x_in, y_out = sem("x_in"), sem("y_out")
        block_ready = sem("block_ready")
        freed_dve, freed_act = sem("freed_dve"), sem("freed_act")
        dve_chain = sem("dve_chain")
        pads_zero = sem("pads_zero")
        squared = sem("squared")
        normed_in = sem("normed_in")
        gn_sd = sem("gn_sd")
        gn_cols = sem("gn_cols")
        vT_out = sem("vT_out")
        keys_strip, queries_strip = sem("keys_strip"), sem("queries_strip")
        scores_in, biased, shifted, exps = sem("scores_in"), sem("biased"), sem("shifted"), sem("exps")
        turned, turned_read = sem("turned"), sem("turned_read")
        values_in = [sem("values_in0"), sem("values_in1")]
        pv_in, recips, recips_masked, out_strip = sem("pv_in"), sem("recips"), sem("recips_masked"), sem("out_strip")
        q_split, k_split, k_chain = sem("q_split"), sem("k_split"), sem("k_chain")
        v_ones = sem("v_ones")
        parts_in = [sem("parts_in0"), sem("parts_in1")]
        max_scores, max_read = sem("max_scores"), sem("max_read")
        max_turned, shift_split, shift_in = sem("max_turned"), sem("shift_split"), sem("shift_in")
        max_chain = sem("max_chain")
        st_ready, exp_done, pv_done = sem("st_ready"), sem("exp_done"), sem("pv_done")
        attn_read, sums_spread, attn_normed, attn_proj, x_updated = (
            sem("attn_read"), sem("sums_spread"), sem("attn_normed"), sem("attn_proj"),
            sem("x_updated"))

        GN, NQ, NK, NV, PROJ, M2, V2, AQ, AK, AV, M3, V3, FFN = range(13)
        reader = {GN: "dve", NQ: "act", NK: "dve", NV: "act", PROJ: "dve", M2: "dve", V2: "act", AQ: "act",
                  AK: "act", AV: "dve", M3: "dve", V3: "act", FFN: "dve"}
        count = {s: 2 if s == GN else NBLK for s in reader}
        ready_base = {s: sum(count[t] for t in range(s)) for s in reader}
        READY = sum(count.values())
        count[GN] = 1
        freed_base = {s: sum(count[t] for t in range(s) if reader[t] == reader[s]) for s in reader}
        FREED = {e: sum(count[t] for t in reader if reader[t] == e) for e in ("dve", "act")}
        freed = {"dve": freed_dve, "act": freed_act}

        def wait_block(eng, b, stage, j):
            eng.wait_ge(block_ready, b * READY + (ready_base[stage] + j + 1))

        def wait_freed(eng, b, stage, j):
            eng.wait_ge(freed[reader[stage]], b * FREED[reader[stage]] + (freed_base[stage] + j + 1))

        def apart(eng):
            eng.sem_inc(paced, 1)

        def blk(t, j):
            return t[:, j * BLK:(j + 1) * BLK]

        block = ctx.enter_context(nc.Block())

        @block.sync
        def _(sp):
            for s in (biased, turned_read, out_strip, exp_done, attn_read, x_updated, max_read, pv_done):
                sp.sem_inc(s, PRIMED)
            sp.sem_inc(shift_in, 16 * PRIMED)
            def load(dst, src):
                sp.dma_start(dst, src).then_inc(weights_in, 16)

            load(C[:, :], consts)
            load(W_qkv[:, :], qkv_wT)
            load(W_proj[:, :], proj_wT)
            load(W_q[:, :], Wq)
            load(W_k[:, :], Wk)
            load(W_v[:, :], Wv)
            load(W_up, WT)
            load(codes, qidx)
            load(scale_blocks[:, :], scales.rearrange("(o n) -> o n", n=P // NF4_BLOCK))
            for n, v in enumerate((proj_b, bq, bk, bo)):
                load(bias_cols[:, n:n + 1], v.rearrange("(c o) -> c o", o=1))
            load(bv_rows[:, :], bass.AP(tensor=bv.tensor, offset=0, ap=[[0, P], [1, P]]))
            sp.wait_ge(setup_dve, 1)
            for g in range(GROUPS):
                for j in range(GH):
                    h = g * GH + j
                    load(W_o[32 * j:32 * j + ADIM, g, :], Wo[h * ADIM:(h + 1) * ADIM, :])
            stage1 = arena[:, 0:3 * 13 * WJ].rearrange("p (t r k) -> p t r k", t=3, r=13)
            sp.wait_ge(table_filled, 3)
            for t, j0 in enumerate((0, QJ, SIDE - QJ)):
                for qi in range(QI):
                    for qj in range(QJ):
                        j = j0 + qj
                        at = first_key(j) - (j0 - PADJ)
                        rx = first_key(j) - j + KSZ - 1
                        q = qi * QJ + qj
                        sp.dma_start(stage1[q:P:QI * QJ, t, :, at:at + KSZ],
                                     rpb[:, :, rx:rx + KSZ]).then_inc(table_cols_in, 16)
            sp.wait_ge(table_cols_in, 16 * 3 * QI * QJ)
            for r, s in enumerate(ROW_TYPES):
                for q in range(QI * QJ):
                    i = QI * s + q // QJ
                    at = first_key(i) - window_row(s)
                    ry = first_key(i) - i + KSZ - 1
                    sp.dma_start(nat_bias[q:P:QI * QJ, r, :, at * WJ:(at + KSZ) * WJ],
                                 stage1[q:P:QI * QJ, :, ry:ry + KSZ, :].rearrange("p t r k -> p t (r k)")
                                 ).then_inc(table_rows_in, 16)
            zeros = arena[0:SIDE, 400:400 + PADJ * P].rearrange("p (k e) -> p k e", k=PADJ)
            v_img = vT_dram.rearrange("(y x) c -> y x c", x=WIDE)
            sp.dma_start(v_img[:, 0:PADJ, :], zeros).then_inc(vpad_out, 16)
            sp.dma_start(v_img[:, PADJ + SIDE:WIDE, :], zeros).then_inc(vpad_out, 16)
            sp.wait_ge(vpad_out, 32)
            sp.wait_ge(table_rows_in, 16 * len(ROW_TYPES) * QI * QJ)

            xv = x.rearrange("b c y x -> b c (y x)")
            yv = out.rearrange("b c y x -> b c (y x)")
            def load_values(row, k):
                for ky in range(WI):
                    src = bass.AP(tensor=vT_dram.tensor, offset=(row + ky) * (WIDE * P),
                                  ap=[[P, WJ], [QJ * P, UNITS], [1, P]])
                    sp.dma_start(VP[ky * WJ:(ky + 1) * WJ, k, :, :], src).then_inc(values_in[k], 16)

            with sp.Fori(0, images) as b:
                sp.dma_start(X[:, :], xv[bass.ds(b, 1)].rearrange("b c t -> (b c) t")).then_inc(x_in, 16)
                wait_freed(sp, b, NV, NBLK - 1)
                for r in range(2):
                    src = VTs[SIDE * r:SIDE * (r + 1), :, :]
                    dst = bass.AP(tensor=vT_dram.tensor, offset=(r * WIDE + PADJ) * P,
                                  ap=[[P, SIDE], [2 * WIDE * P, 28], [1, P]])
                    sp.dma_start(dst, src).then_inc(vT_out, 16)
                sp.wait_ge(vT_out, b * 32 + 32)
                sp.wait_ge(pads_zero, b * 3 + 3)

                load_values(window_row(0), 0)
                load_values(window_row(1), 1)
                with sp.Fori(1, STRIPS // 2 - 1) as t:
                    for k in range(2):
                        sp.wait_ge(pv_in, b * STRIPS + (t * 2 + (k - 1)))
                        apart(sp)
                        load_values(t * 4 + (2 * k - 3), k)
                for k in range(2):
                    s = STRIPS - 2 + k
                    sp.wait_ge(pv_in, b * STRIPS + (s - 1))
                    load_values(window_row(s), k)

                sp.wait_ge(q_split, b + 1)
                sp.wait_ge(k_split, b + 1)
                for g in range(GROUPS):
                    for h in range(GH):
                        c0 = (g * GH + h) * ADIM
                        for n in range(len(Q_PARTS)):
                            sp.dma_start(QP[n * ADIM:(n + 1) * ADIM, g, h, 0:TOK],
                                         q_parts[c0:c0 + ADIM, Q_PARTS[n], :]).then_inc(parts_in[g], 16)
                            sp.dma_start(KP[n * ADIM:(n + 1) * ADIM, g, h, :],
                                         k_parts[c0:c0 + ADIM, K_PARTS[n], :]).then_inc(parts_in[g], 16)
                for g in range(GROUPS):
                    sp.wait_ge(shift_split, b * (3 * GROUPS) + (3 * g + 3))
                    for h in range(GH):
                        for n in range(3):
                            sp.dma_start(QP[ROWS + n:ROWS + n + 1, g, h, :].rearrange("p (c t) -> p c t", t=P),
                                         shift_parts[h * CHUNKS:(h + 1) * CHUNKS, n, :]).then_inc(shift_in, 16)
                for j in range(NBLK):
                    wait_freed(sp, b, FFN, j)
                    sp.dma_start(yv[bass.ds(b, 1)].rearrange("b c t -> (b c) t")[:, j * BLK:(j + 1) * BLK],
                                 blk(X, j)).then_inc(y_out, 16)
                sp.wait_ge(y_out, b * (16 * NBLK) + 16 * NBLK)
                apart(sp)

        @block.gpsimd
        def _(pool):
            pool.wait_ge(weights_in, 16 * 22)
            nc.gpsimd.memset(ones96[:, :], 1.0).then_inc(setup_pool, 1)
            pool.wait_ge(setup_pool, 1)
            nc.gpsimd.memset(KP[96:128, :, :, :], 1.0).then_inc(setup_pool, 1)
            pool.wait_ge(setup_pool, 2)

            with pool.Fori(0, images) as b:
                nc.gpsimd.memset(Kn, 0.0).then_inc(pads_zero, 1)
                pool.wait_ge(pads_zero, b * 3 + 1)
                apart(pool)
                nc.gpsimd.memset(PT[64:96, :, :, :], 0.0).then_inc(pads_zero, 1)
                nc.gpsimd.memset(VP[64:96, :, :, :], 0.0).then_inc(pads_zero, 1)
                pool.wait_ge(pads_zero, b * 3 + 3)
                apart(pool)

                def spread_queries(tok0, k):
                    for i in range(QI):
                        src = Qn[:, bass.ds(tok0 + i * SIDE, SIDE)] if not isinstance(tok0, int) else \
                            Qn[:, tok0 + i * SIDE:tok0 + (i + 1) * SIDE]
                        dst = QB[:, k, :, :].rearrange("p u (h i j) -> p u h i j", h=GH, i=QI)[:, :, :, i, :]
                        src = src.rearrange("p (u o j) -> p u o j", o=1, j=QJ).to_broadcast([P, UNITS, GH, QJ])
                        m = head_mask.rearrange("p (o h a) -> p o h a", o=1, a=1).to_broadcast([P, UNITS, GH, QJ])
                        nc.gpsimd.tensor_tensor(dst, src, m, ALU.mult).then_inc(queries_strip, 1)

                def subtract_max(n, k):
                    pool.wait_ge(biased, (n + 1) * 6 + PRIMED)
                    m = NM[:, k, 0:UNITS].rearrange("p (u o) -> p u o", o=1).to_broadcast([P, UNITS, KEYS])
                    nc.gpsimd.tensor_tensor(SC[:, k, :, :], SC[:, k, :, :], m, ALU.add).then_inc(shifted, 1)

                def mask_recips(n, k):
                    pool.wait_ge(recips, n + 1)
                    r = RS[:, k, :].rearrange("p (u h q) -> p u h q", u=UNITS, h=GH)
                    m = head_mask.rearrange("p (o h a) -> p o h a", o=1, a=1).to_broadcast([P, UNITS, GH, QI * QJ])
                    nc.gpsimd.tensor_tensor(RM[:, k, :].rearrange("p (u h q) -> p u h q", u=UNITS, h=GH), r, m,
                                            ALU.mult).then_inc(recips_masked, 1)

                wait_freed(pool, b, NQ, NBLK - 1)
                apart(pool)
                base = b * STRIPS

                def strip(s, k, first):
                    n = base + s
                    if not (isinstance(s, int) and s < 2):
                        pool.wait_ge(scores_in, n - 1)
                    spread_queries(s * (QI * SIDE), k)
                    subtract_max(n, k)
                    if not first:
                        mask_recips(n - 1, 1 - k)

                strip(0, 0, True)
                strip(1, 1, False)
                with pool.Fori(1, STRIPS // 2) as t:
                    strip(t * 2, 0, False)
                    strip(t * 2 + 1, 1, False)
                mask_recips(base + (STRIPS - 1), 1)

                wait_freed(pool, b, AK, NBLK - 1)
                apart(pool)
                chain = [0]

                def own(ins):
                    ins.then_inc(k_chain, 1)
                    chain[0] += 1
                    pool.wait_ge(k_chain, b * 3 + chain[0])
                    apart(pool)

                own(nc.gpsimd.tensor_copy(k_parts[:, 0, :], k_full))
                own(nc.gpsimd.tensor_tensor(k_rest, k_full, k_parts[:, 0, :], ALU.subtract))
                own(nc.gpsimd.tensor_copy(k_parts[:, 1, :], k_rest))
                nc.gpsimd.tensor_tensor(k_parts[:, 2, :], k_rest, k_parts[:, 1, :],
                                        ALU.subtract).then_inc(k_split, 1)
                nc.gpsimd.memset(VA[:, 0:CHUNKS - 1, :, ADIM:32], 1.0).then_inc(v_ones, 1)
                nc.gpsimd.memset(VA[0:LAST, CHUNKS - 1, :, ADIM:32], 1.0).then_inc(v_ones, 1)
                pool.wait_ge(v_ones, b * 3 + 2)
                apart(pool)
                nc.gpsimd.memset(VA[LAST:P, CHUNKS - 1, :, :], 0.0).then_inc(v_ones, 1)
                pool.wait_ge(v_ones, b * 3 + 3)
                wait_freed(pool, b, FFN, NBLK - 1)

        @block.tensor
        def _(pe):
            mm = nc.tensor.matmul

            pe.wait_ge(setup_dve, len(NF4) + 3)
            pe.wait_ge(weights_in, 16 * 22)
            pe.wait_ge(setup_pool, 2)
            mm(PS[:, 0, 0:P], normed[:, 0:P], W_up, start=True, stop=True).then_inc(setup_pe, 1)
            pe.wait_ge(setup_dve, len(NF4) + 4)

            with pe.Fori(0, images) as b:
                for n in range(2):
                    pe.wait_ge(gn_cols, b * 3 + (n + 1))
                    mm(PS[:, 7, n:n + 1], group_w, gn[:, 3 * n:3 * n + 1], start=True,
                       stop=True).then_inc(block_ready, 1)
                pe.wait_ge(gn_cols, b * 3 + 3)
                for j in range(NBLK):
                    mm(PS[:, j, 0:BLK], W_qkv[:, 0:P], blk(XN, j), start=True, stop=True).then_inc(block_ready, 1)
                for j in range(NBLK):
                    wait_freed(pe, b, NQ, j)
                    mm(PS[:, j, 0:BLK], W_qkv[:, P:2 * P], blk(XN, j), start=True, stop=True).then_inc(block_ready, 1)
                for j in range(NBLK):
                    wait_freed(pe, b, NK, j)
                    for c in range(4):
                        t0 = (4 * j + c) * VROW
                        m = mm(PS[0:VROW, j, c * P:(c + 1) * P], XN[:, t0:t0 + VROW], W_qkv[:, 2 * P:3 * P],
                               start=True, stop=True)
                    m.then_inc(block_ready, 1)
                wait_freed(pe, b, NV, NBLK - 1)
                pe.wait_ge(pads_zero, b * 3 + 3)

                base = b * STRIPS
                s_at = [(0, u) if u < 5 else (1, u - 5) if u < 10 else (2, u - 10) for u in range(UNITS)]

                def scores(n, k):
                    pe.wait_ge(keys_strip, n + 1)
                    pe.wait_ge(queries_strip, n * 2 + 2)
                    pe.wait_ge(biased, n * 6 + PRIMED)
                    apart(pe)
                    win = KS[:, k, :].rearrange("p (y x) -> p y x", x=WIDE)
                    for u in range(UNITS):
                        bk_, at = s_at[u]
                        for g in range(4):
                            r = slice(32 * g, 32 * g + 32)
                            m = mm(PS[r, bk_, at * KEYS:(at + 1) * KEYS], QB[r, k, u, :],
                                   win[r, :, u * QJ:u * QJ + WJ], start=True, stop=True,
                                   tile_position=(32 * g, 32 * g))
                    m.then_inc(scores_in, 1)

                def turn_and_sum(n, k):
                    pe.wait_ge(exps, n + 1)
                    for c in range(4):
                        pe.wait_ge(turned_read, n * 4 + max(c - 1, 0) + PRIMED)
                        for u in range(4 * c, min(4 * c + 4, UNITS)):
                            m = nc.tensor.transpose(PS[0:KEYS, 3 + c % 2, (u % 4) * P:(u % 4 + 1) * P],
                                                    SC[:, k, u, :], ident)
                        m.then_inc(turned, 1)
                    pe.wait_ge(turned_read, n * 4 + 4 + PRIMED)
                    pe.wait_ge(out_strip, n * 3 + PRIMED)
                    for g in range(4):
                        mm(PS[32 * g:32 * g + 32, 7, 0:BLK], ones96[0:KPAD, :], PT[0:KPAD, k, :, 32 * g:32 * g + 32],
                           start=True, stop=True, tile_position=(0, 32 * g))

                def values(n, k, visit):
                    pe.wait_ge(values_in[k], visit)
                    for u in range(UNITS):
                        for g in range(4):
                            m = mm(PS[32 * g:32 * g + 32, 6, 32 * u:32 * u + 32],
                                   VP[0:KPAD, k, u, 32 * g:32 * g + 32], PT[0:KPAD, k, u, 32 * g:32 * g + 32],
                                   start=True, stop=True, tile_position=(0, 32 * g))
                    m.then_inc(pv_in, 1)

                VIS = 16 * WI
                per = STRIPS // 2 * VIS
                scores(base, 0)
                scores(base + 1, 1)
                turn_and_sum(base, 0)
                values(base, 0, b * per + VIS)
                with pe.Fori(1, STRIPS // 2) as t:
                    scores(base + t * 2, 0)
                    turn_and_sum(base + (t * 2 - 1), 1)
                    values(base + (t * 2 - 1), 1, b * per + t * VIS)
                    scores(base + (t * 2 + 1), 1)
                    turn_and_sum(base + t * 2, 0)
                    values(base + t * 2, 0, b * per + t * VIS + VIS)
                turn_and_sum(base + (STRIPS - 1), 1)
                values(base + (STRIPS - 1), 1, b * per + per)
                pe.wait_ge(out_strip, b * (3 * STRIPS) + 3 * STRIPS + PRIMED)

                for j in range(NBLK):
                    mm(PS[:, j, 0:BLK], W_proj[:, :], blk(On, j), start=True, stop=True).then_inc(block_ready, 1)

                def layer_norm(mean_stage, var_stage, before, visit):
                    for j in range(NBLK):
                        wait_freed(pe, b, before, j) if before is not None else None
                        mm(PS[:, j, 0:BLK], mean_w, blk(X, j), start=True, stop=True).then_inc(block_ready, 1)
                    for j in range(NBLK):
                        wait_freed(pe, b, mean_stage, j)
                        pe.wait_ge(squared, b * (2 * NBLK) + (visit * NBLK + j + 1))
                        mm(PS[:, j, 0:BLK], mean_w, blk(SQ, j), start=True, stop=True).then_inc(block_ready, 1)

                layer_norm(M2, V2, PROJ, 0)
                for j in range(NBLK):
                    wait_freed(pe, b, V2, j)
                    pe.wait_ge(normed_in, b * (2 * NBLK) + (j + 1))
                    mm(PS[:, j, 0:BLK], W_q[:, :], blk(XN, j), start=True, stop=True).then_inc(block_ready, 1)
                for j in range(NBLK):
                    wait_freed(pe, b, AQ, j)
                    mm(PS[:, j, 0:BLK], W_k[:, :], blk(XN, j), start=True, stop=True).then_inc(block_ready, 1)
                for j in range(NBLK):
                    wait_freed(pe, b, AK, j)
                    for c in range(4 * j, min(4 * j + 4, CHUNKS)):
                        n = LAST if c == CHUNKS - 1 else P
                        m = mm(PS[0:n, j, (c % 4) * P:(c % 4 + 1) * P], XN[:, c * P:c * P + n], W_v[:, :],
                               start=True, stop=True)
                    m.then_inc(block_ready, 1)
                wait_freed(pe, b, AV, NBLK - 1)

                def attention(exp_g, max_g):
                    if exp_g is not None:
                        pe.wait_ge(shift_in, b * (GROUPS * 16 * 3 * GH) + (exp_g + 1) * 16 * 3 * GH + 16 * PRIMED)
                        pe.wait_ge(v_ones, b * 3 + 3)
                    if max_g is not None:
                        pe.wait_ge(parts_in[max_g], b * (16 * 2 * GH * len(Q_PARTS)) + 16 * 2 * GH * len(Q_PARTS))
                    apart(pe)
                    with pe.Fori(0, NBLK) as i:
                        e = b * (GROUPS * NBLK) + (i + exp_g * NBLK) if exp_g is not None else None
                        mi = b * (GROUPS * NBLK) + (i + max_g * NBLK) if max_g is not None else None

                        def weigh(c):
                            pe.wait_ge(exp_done, e * (2 * CHUNKS) + (2 * c + 2) + PRIMED)
                            if c == 0:
                                pe.wait_ge(attn_read, e + PRIMED)
                            for h in range(GH):
                                m = mm(PS[32 * h:32 * h + 32, 6, 0:BLK], VA[:, c, exp_g * GH + h, :],
                                       PB[:, c % 2, h, :], start=(c == 0), stop=(c == CHUNKS - 1),
                                       tile_position=(0, 32 * h))
                            m.then_inc(pv_done, 1)

                        for c in range(CHUNKS):
                            n = LAST if c == CHUNKS - 1 else P
                            if exp_g is not None:
                                for p in range(2):
                                    if c > 0:
                                        pe.wait_ge(exp_done, e * (2 * CHUNKS) + (2 * c + p - 1) + PRIMED)
                                        if n < P:
                                            apart(pe)
                                    elif p == 0:
                                        pe.wait_ge(exp_done, e * (2 * CHUNKS) + PRIMED)
                                    for h in (2 * p, 2 * p + 1):
                                        m = mm(PS[0:n, h, 0:BLK], KP[0:ROWSM, exp_g, h, c * P:c * P + n],
                                               QP[0:ROWSM, exp_g, h, bass.ds(i * BLK, BLK)], start=True, stop=True)
                                    m.then_inc(st_ready, 1)
                            if max_g is not None:
                                for h in range(GH):
                                    u = c * GH + h
                                    if u >= 2:
                                        pe.wait_ge(max_read, mi * (CHUNKS * GH) + (u - 1) + PRIMED)
                                        if n < P:
                                            apart(pe)
                                    elif u == 0:
                                        pe.wait_ge(max_read, mi * (CHUNKS * GH) + PRIMED)
                                    mm(PS[0:n, 4 + u % 2, 0:BLK], QP[0:ROWS, max_g, h, c * P:c * P + n],
                                       KP[0:ROWS, max_g, h, bass.ds(i * BLK, BLK)], start=True,
                                       stop=True).then_inc(max_scores, 1)
                            if exp_g is not None and c > 0:
                                weigh(c - 1)
                        if exp_g is not None:
                            weigh(CHUNKS - 1)
                            pe.wait_ge(attn_read, e + 1 + PRIMED)
                            pe.wait_ge(x_updated, e + PRIMED)
                            mm(PS[:, 7, 0:BLK], pick_sum, tail[:, 0, :], start=True, stop=True).then_inc(sums_spread, 1)
                            pe.wait_ge(attn_normed, e * 2 + 2)
                            mm(PS[:, 7, 0:BLK], W_o[:, exp_g, :], normed[:, :], start=True,
                               stop=True).then_inc(attn_proj, 1)
                    if exp_g is not None:
                        pe.wait_ge(x_updated, b * (GROUPS * NBLK) + (exp_g + 1) * NBLK + PRIMED)
                    if max_g is not None:
                        pe.wait_ge(max_chain, b * (GROUPS * NBLK) + (max_g + 1) * NBLK)
                        nc.tensor.transpose(PS[0:GH * CHUNKS, 7, 0:P], maxes[:, 1, :], ident).then_inc(max_turned, 1)
                        pe.wait_ge(shift_split, b * (3 * GROUPS) + (3 * max_g + 1))

                attention(None, 0)
                attention(0, 1)
                attention(1, None)

                layer_norm(M3, V3, None, 1)
                for j in range(NBLK):
                    wait_freed(pe, b, V3, j)
                    pe.wait_ge(normed_in, b * (2 * NBLK) + (NBLK + j + 1))
                    mm(PS[:, j, 0:BLK], W_ffn[:, :], blk(XN, j), start=True, stop=True).then_inc(block_ready, 1)
                wait_freed(pe, b, FFN, NBLK - 1)

        @block.scalar
        def _(act):
            act.wait_ge(weights_in, 16 * 22)
            with act.Fori(0, images) as b:
                wait_block(act, b, GN, 1)
                nc.scalar.activation(gn[:, 7:8], PS[:, 7, 1:2], ACT.Sqrt, bias=eps5).then_inc(gn_sd, 1)
                for j in range(NBLK):
                    wait_block(act, b, NQ, j)
                    nc.scalar.activation(blk(Qn, j), PS[:, j, 0:BLK], ACT.Copy,
                                         scale=float(NDIM) ** -0.5).then_inc(freed_act, 1)
                for j in range(NBLK):
                    wait_block(act, b, NV, j)
                    nc.scalar.activation(VTs[0:VROW, 4 * j:4 * j + 4, :].rearrange("p c e -> p (c e)"),
                                         PS[0:VROW, j, :], ACT.Copy).then_inc(freed_act, 1)

                base = b * STRIPS
                wait_freed(act, b, NK, NBLK - 1)
                act.wait_ge(pads_zero, b * 3 + 3)

                def keys(n, row, k, first):
                    if not first:
                        act.wait_ge(scores_in, n - 1)
                    src = Kn[:, bass.ds(row * WIDE, WI * WIDE)] if not isinstance(row, int) else \
                        Kn[:, row * WIDE:(row + WI) * WIDE]
                    nc.scalar.activation(KS[:, k, :], src, ACT.Copy).then_inc(keys_strip, 1)

                def exponentials(n, k):
                    act.wait_ge(shifted, n + 1)
                    v = SC[:, k, :, :].rearrange("p u k -> p (u k)")
                    nc.scalar.activation(v, v, ACT.Exp).then_inc(exps, 1)

                def read_turned(n, k, first):
                    for c in range(4):
                        act.wait_ge(turned, n * 4 + (c + 1))
                        if c == 0 and not first:
                            act.wait_ge(pv_in, n - 1)
                        u0, u1 = 4 * c, min(4 * c + 4, UNITS)
                        nc.scalar.activation(PT[0:KEYS, k, u0:u1, :].rearrange("p u e -> p (u e)"),
                                             PS[0:KEYS, 3 + c % 2, 0:(u1 - u0) * P], ACT.Copy).then_inc(turned_read, 1)

                keys(base, window_row(0), 0, True)
                exponentials(base, 0)
                keys(base + 1, window_row(1), 1, True)
                read_turned(base, 0, True)
                exponentials(base + 1, 1)
                with act.Fori(1, STRIPS // 2 - 1) as t:
                    keys(base + t * 2, t * 4 - 3, 0, False)
                    read_turned(base + (t * 2 - 1), 1, False) 
                    exponentials(base + t * 2, 0)
                    keys(base + (t * 2 + 1), t * 4 - 1, 1, False)
                    read_turned(base + t * 2, 0, False)
                    exponentials(base + (t * 2 + 1), 1)
                s = STRIPS - 2
                keys(base + s, window_row(s), 0, False)
                read_turned(base + (s - 1), 1, False)
                exponentials(base + s, 0)
                keys(base + (s + 1), window_row(s + 1), 1, False)
                read_turned(base + s, 0, False)
                exponentials(base + (s + 1), 1)
                read_turned(base + (s + 1), 1, False)

                def layer_norm(mean_stage, var_stage):
                    for j in range(NBLK):
                        wait_freed(act, b, mean_stage, j)
                        nc.scalar.activation(blk(SQ, j), blk(XN, j), ACT.Square).then_inc(squared, 1)
                    for j in range(NBLK):
                        wait_block(act, b, var_stage, j)
                        nc.scalar.activation(blk(SD, j), PS[:, j, 0:BLK], ACT.Sqrt,
                                             bias=eps5).then_inc(freed_act, 1)

                layer_norm(M2, V2)
                for stage, full, col in ((AQ, q_full, 1), (AK, k_full, 2)):
                    for j in range(NBLK):
                        wait_block(act, b, stage, j)
                        ins = nc.scalar.activation(blk(full, j), PS[:, j, 0:BLK], ACT.Identity,
                                                   bias=bias_cols[:, col:col + 1])
                        ins.then_inc(freed_act, 1)

                def exps_of(g):
                    with act.Fori(0, NBLK) as i:
                        e = b * (GROUPS * NBLK) + (i + g * NBLK)
                        for c in range(CHUNKS):
                            n = LAST if c == CHUNKS - 1 else P
                            for p in range(2):
                                act.wait_ge(st_ready, e * (2 * CHUNKS) + (2 * c + p + 1))
                                if p == 0 and c != 1:
                                    act.wait_ge(pv_done, e * CHUNKS + max(c - 1, 0) + PRIMED)
                                nc.scalar.activation(PB[0:n, c % 2, 2 * p:2 * p + 2, :], PS[0:n, 2 * p:2 * p + 2, 0:BLK],
                                                     ACT.Exp, scale=float(ADIM) ** -0.5).then_inc(exp_done, 1)

                exps_of(0)
                exps_of(1)
                layer_norm(M3, V3)

        @block.vector
        def _(dve):
            V = nc.vector
            V.memset(W_o[:, :, :], 0.0).then_inc(setup_dve, 1)
            V.memset(nat_bias[:, :, :, :], MASKED).then_inc(table_filled, 1)
            V.memset(arena[:, 0:3 * 13 * WJ], MASKED).then_inc(table_filled, 1)
            V.memset(arena[:, 400:800], 0.0).then_inc(table_filled, 1)
            V.memset(maxes[:, 0, :], 0.0).then_inc(setup_dve, 1)
            dve.wait_ge(weights_in, 16 * 22)
            w, term = normed[:, 0:P], tail[:, 0, 0:P]
            for k, value in enumerate(NF4):
                V.tensor_scalar(term, codes, float(k), value, ALU.is_equal, ALU.mult).then_inc(dve_chain, 1)
                dve.wait_ge(dve_chain, k + 1)
                if k == 0:
                    V.tensor_copy(w, term).then_inc(setup_dve, 1)
                else:
                    V.tensor_tensor(w, w, term, ALU.add).then_inc(setup_dve, 1)
                dve.wait_ge(setup_dve, k + 3)
            wv = w.rearrange("p (n e) -> p n e", e=NF4_BLOCK)
            s = scale_blocks[:, :].rearrange("p (n o) -> p n o", o=1).to_broadcast([P, P // NF4_BLOCK, NF4_BLOCK])
            V.tensor_tensor(wv, wv, s, ALU.mult).then_inc(setup_dve, 1)
            dve.wait_ge(setup_pe, 1)
            V.tensor_copy(W_ffn[:, :], PS[:, 0, 0:P]).then_inc(setup_dve, 1)
            dve.wait_ge(table_rows_in, 16 * len(ROW_TYPES) * QI * QJ)
            dve.wait_ge(vpad_out, 32)

            with dve.Fori(0, images) as b:
                chain = [0]

                def own(ins, alone=False):
                    ins.then_inc(dve_chain, 1)
                    chain[0] += 1
                    dve.wait_ge(dve_chain, b * OWN + (len(NF4) + chain[0]))
                    if alone:
                        apart(dve)

                dve.wait_ge(x_in, b * 16 + 16)
                for j in range(NBLK):
                    ins = V.bn_stats(stats[:, j, :], blk(X, j))
                own(ins, alone=True)
                V.bn_aggr(gn[:, 0:2], stats[:, :, :]).then_inc(gn_cols, 1)
                wait_block(dve, b, GN, 0)
                V.tensor_copy(gn[:, 4:5], PS[:, 7, 0:1]).then_inc(freed_dve, 1)
                wait_freed(dve, b, GN, 0)
                own(V.tensor_tensor(gn[:, 5:6], gn[:, 0:1], gn[:, 4:5], ALU.subtract))
                own(V.tensor_tensor(gn[:, 6:7], gn[:, 5:6], gn[:, 5:6], ALU.mult))
                V.tensor_tensor(gn[:, 3:4], gn[:, 6:7], gn[:, 1:2], ALU.add).then_inc(gn_cols, 1)
                dve.wait_ge(gn_sd, b + 1)
                own(V.reciprocal(gn[:, 8:9], gn[:, 7:8]))
                V.tensor_scalar(XN, X[:, :], gn[:, 4:5], gn[:, 8:9], ALU.subtract, ALU.mult).then_inc(gn_cols, 1)
                dve.wait_ge(pads_zero, b * 3 + 3)
                k_img = Kn.rearrange("p (y x) -> p y x", x=WIDE)
                rows = BLK // SIDE
                for j in range(NBLK):
                    wait_block(dve, b, NK, j)
                    V.tensor_copy(k_img[:, rows * j:rows * (j + 1), PADJ:PADJ + SIDE],
                                  PS[:, j, 0:BLK].rearrange("p (y x) -> p y x", x=SIDE)).then_inc(freed_dve, 1)

                base = b * STRIPS

                def add_bias(n, k, row_type, first):
                    dve.wait_ge(scores_in, n + 1)
                    if not first:
                        dve.wait_ge(turned, (n - 1) * 4)
                    for bk_, u0, u1, kind in ((0, 0, 1, 0), (0, 1, 5, 1), (1, 5, 10, 1), (2, 10, 13, 1), (2, 13, 14, 2)):
                        at = (u0 - (0, 5, 10)[bk_]) * KEYS
                        m = u1 - u0
                        V.tensor_tensor(
                            SC[:, k, u0:u1, :], PS[:, bk_, at:at + m * KEYS].rearrange("p (u k) -> p u k", u=m),
                            nat_bias[:, row_type, kind:kind + 1, :].to_broadcast([P, m, KEYS]),
                            ALU.add).then_inc(biased, 1)
                    dve.wait_ge(biased, n * 6 + 5 + PRIMED)
                    V.tensor_reduce(NM[:, k, 0:UNITS], SC[:, k, :, :], AX.X, ALU.max, negate=True).then_inc(biased, 1)

                def finish(n, k, tok0):
                    dve.wait_ge(pv_in, n + 1)
                    V.reciprocal(RS[:, k, :], PS[:, 7, 0:BLK]).then_inc(recips, 1)
                    dve.wait_ge(recips_masked, n + 1)
                    V.tensor_tensor(PVM, PS[:, 6, 0:BLK], RM[:, k, :], ALU.mult).then_inc(out_strip, 1)
                    dve.wait_ge(out_strip, n * 3 + 1 + PRIMED)
                    v = PVM.rearrange("p (u h i j) -> p i u j h", u=UNITS, h=GH, i=QI)
                    for i in range(QI):
                        o = On[:, tok0 + i * SIDE:tok0 + (i + 1) * SIDE] if isinstance(tok0, int) else \
                            On[:, bass.ds(tok0 + i * SIDE, SIDE)]
                        V.tensor_reduce(o.rearrange("p (u j) -> p u j", u=UNITS), v[:, i], AX.X,
                                        ALU.add).then_inc(out_strip, 1)

                ROW = QI * SIDE
                add_bias(base, 0, 0, True)
                add_bias(base + 1, 1, 1, True)
                finish(base, 0, 0)
                with dve.Fori(1, STRIPS // 2 - 1) as t:
                    add_bias(base + t * 2, 0, 2, False)
                    finish(base + (t * 2 - 1), 1, t * (2 * ROW) - ROW)
                    add_bias(base + (t * 2 + 1), 1, 2, False)
                    finish(base + t * 2, 0, t * (2 * ROW))
                s = STRIPS - 2
                add_bias(base + s, 0, 3, False)
                finish(base + (s - 1), 1, (s - 1) * ROW)
                add_bias(base + (s + 1), 1, 4, False)
                finish(base + s, 0, s * ROW)
                finish(base + (s + 1), 1, (s + 1) * ROW)

                for j in range(NBLK):
                    wait_block(dve, b, PROJ, j)
                    V.scalar_tensor_tensor(out=blk(X, j), in0=PS[:, j, 0:BLK], scalar=bias_cols[:, 0:1],
                                           in1=blk(X, j), op0=ALU.add, op1=ALU.add).then_inc(freed_dve, 1)

                def layer_norm(mean_stage, var_stage):
                    for j in range(NBLK):
                        wait_block(dve, b, mean_stage, j)
                        V.tensor_tensor(blk(XN, j), blk(X, j), PS[:, j, 0:BLK], ALU.subtract).then_inc(freed_dve, 1)
                    for j in range(NBLK):
                        wait_freed(dve, b, var_stage, j)
                        own(V.reciprocal(blk(SD, j), blk(SD, j)))
                        V.tensor_tensor(blk(XN, j), blk(XN, j), blk(SD, j), ALU.mult).then_inc(normed_in, 1)

                layer_norm(M2, V2)
                wait_freed(dve, b, AQ, NBLK - 1)
                own(V.tensor_copy(q_parts[:, 0, :], q_full))
                own(V.tensor_tensor(q_rest, q_full, q_parts[:, 0, :], ALU.subtract))
                own(V.tensor_copy(q_parts[:, 1, :], q_rest))
                V.tensor_tensor(q_parts[:, 2, :], q_rest, q_parts[:, 1, :], ALU.subtract).then_inc(q_split, 1)
                for j in range(NBLK):
                    wait_block(dve, b, AV, j)
                    m = min(4, CHUNKS - 4 * j)
                    n = LAST if m == 1 else P
                    V.tensor_tensor(VA[0:n, 4 * j:4 * j + m, :, 0:ADIM],
                                    PS[0:n, j, 0:m * P].rearrange("p (c h e) -> p c h e", c=m, h=AHEADS),
                                    bv_rows[0:n, :].rearrange("p (o h e) -> p o h e", o=1, h=AHEADS)
                                    .to_broadcast([n, m, AHEADS, ADIM]), ALU.add).then_inc(freed_dve, 1)

                def attention(exp_g, max_g):
                    if max_g is not None:
                        own(V.memset(maxes[:, 1, :], -3.0e38), alone=True)
                    apart(dve)
                    with dve.Fori(0, NBLK) as i:
                        e = b * (GROUPS * NBLK) + (i + exp_g * NBLK) if exp_g is not None else None
                        mi = b * (GROUPS * NBLK) + (i + max_g * NBLK) if max_g is not None else None
                        if max_g is not None:
                            for c in range(CHUNKS):
                                n = LAST if c == CHUNKS - 1 else P
                                for h in range(GH):
                                    u = c * GH + h
                                    dve.wait_ge(max_scores, mi * (CHUNKS * GH) + (u + 1))
                                    at = h * CHUNKS + c
                                    V.tensor_reduce(maxes[0:n, 0, at:at + 1], PS[0:n, 4 + u % 2, 0:BLK], AX.X,
                                                    ALU.max).then_inc(max_read, 1)
                            dve.wait_ge(max_read, mi * (CHUNKS * GH) + CHUNKS * GH + PRIMED)
                            V.tensor_tensor(maxes[:, 1, :], maxes[:, 1, :], maxes[:, 0, :],
                                            ALU.max).then_inc(max_chain, 1)
                            dve.wait_ge(max_chain, mi + 1)
                        if exp_g is not None:
                            dve.wait_ge(pv_done, e * CHUNKS + CHUNKS + PRIMED)
                            V.tensor_copy(tail[:, 0, :], PS[:, 6, 0:BLK]).then_inc(attn_read, 1)
                            dve.wait_ge(sums_spread, e + 1)
                            V.reciprocal(tail[:, 1, :], PS[:, 7, 0:BLK]).then_inc(attn_normed, 1)
                            dve.wait_ge(attn_normed, e * 2 + 1)
                            dve.wait_ge(attn_read, e + 1 + PRIMED)
                            V.tensor_tensor(normed[:, :], tail[:, 0, :], tail[:, 1, :], ALU.mult).then_inc(attn_normed, 1)
                            dve.wait_ge(attn_proj, e + 1)
                            xb = X[:, bass.ds(i * BLK, BLK)]
                            if exp_g == 0:
                                ins = V.scalar_tensor_tensor(out=xb, in0=PS[:, 7, 0:BLK], scalar=bias_cols[:, 3:4],
                                                             in1=xb, op0=ALU.add, op1=ALU.add)
                            else:
                                ins = V.tensor_tensor(xb, xb, PS[:, 7, 0:BLK], ALU.add)
                            ins.then_inc(x_updated, 1)
                    if exp_g is not None:
                        dve.wait_ge(x_updated, b * (GROUPS * NBLK) + (exp_g + 1) * NBLK + PRIMED)
                    if max_g is not None:
                        rows = GH * CHUNKS
                        done = b * GROUPS + max_g
                        dve.wait_ge(max_turned, done + 1)
                        dve.wait_ge(shift_in, done * (16 * 3 * GH) + 16 * PRIMED)
                        own(V.tensor_scalar(shift[0:rows, 0, :], PS[0:rows, 7, 0:P], -1.0, None, ALU.mult))
                        V.tensor_copy(shift_parts[0:rows, 0, :], shift[0:rows, 0, :]).then_inc(shift_split, 1)
                        dve.wait_ge(shift_split, done * 3 + 1)
                        own(V.tensor_tensor(shift[0:rows, 1, :], shift[0:rows, 0, :], shift_parts[0:rows, 0, :],
                                            ALU.subtract))
                        V.tensor_copy(shift_parts[0:rows, 1, :], shift[0:rows, 1, :]).then_inc(shift_split, 1)
                        dve.wait_ge(shift_split, done * 3 + 2)
                        V.tensor_tensor(shift_parts[0:rows, 2, :], shift[0:rows, 1, :], shift_parts[0:rows, 1, :],
                                        ALU.subtract).then_inc(shift_split, 1)

                attention(None, 0)
                attention(0, 1)
                attention(1, None)

                layer_norm(M3, V3)
                for j in range(NBLK):
                    wait_block(dve, b, FFN, j)
                    V.tensor_tensor(blk(X, j), blk(X, j), PS[:, j, 0:BLK], ALU.add).then_inc(freed_dve, 1)
                assert chain[0] == OWN, chain


def kernel(x, L0_conv_qkv_w, L0_conv_rpb, L0_conv_proj_w, L0_conv_proj_b, L1_attn_Wq, L1_attn_bq, L1_attn_Wk,
           L1_attn_bk, L1_attn_Wv, L1_attn_bv, L1_attn_Wo, L1_attn_bo, L1_ffn_qidx, L1_ffn_scales, L1_ffn_W):
    import concourse.bacc as bacc
    from concourse.bass_utils import run_bass_kernel_spmd

    args = {
        "x": x, "consts": shape_constants(), "qkv_wT": np.asarray(L0_conv_qkv_w).T, "rpb": L0_conv_rpb,
        "proj_wT": np.asarray(L0_conv_proj_w).T, "proj_b": L0_conv_proj_b, "Wq": L1_attn_Wq, "bq": L1_attn_bq,
        "Wk": L1_attn_Wk, "bk": L1_attn_bk, "Wv": L1_attn_Wv, "bv": L1_attn_bv, "Wo": L1_attn_Wo,
        "bo": L1_attn_bo, "qidx": L1_ffn_qidx, "scales": L1_ffn_scales, "WT": np.asarray(L1_ffn_W).T,
    }
    nc = bacc.Bacc("TRN2", target_bir_lowering=False, num_devices=1)
    arrays, aps = {}, {}
    for name, a in args.items():
        a = np.ascontiguousarray(a)
        arrays[f"in_{name}"] = a
        aps[name] = nc.dram_tensor(f"in_{name}", a.shape, mybir.dt.from_np(a.dtype), kind="ExternalInput").ap()
    aps["out"] = nc.dram_tensor("out_y", arrays["in_x"].shape, F32, kind="ExternalOutput").ap()
    hybrid_block(nc, arrays["in_x"].shape[0], **aps)
    r = run_bass_kernel_spmd(nc, [arrays], core_ids=[0])
    return r.results[0]["out_y"]
```

```python
from contextlib import ExitStack

import numpy as np

import concourse.bass as bass
from concourse import mybir

F32 = mybir.dt.float32
BF16 = mybir.dt.bfloat16
I32 = mybir.dt.int32
ALU = mybir.AluOpType
ACT = mybir.ActivationFunctionType
AX = mybir.AxisListType

P = 128
SIDE = 56
TOK = SIDE * SIDE
BLK = 448
NBLK = TOK // BLK

KSZ = 7
NHEADS = 16
NDIM = P // NHEADS
QI, QJ = 2, 4
WI, WJ = QI + KSZ - 1, QJ + KSZ - 1
KEYS = WI * WJ
UNITS = SIDE // QJ
STRIPS = SIDE // QI
PADJ = KSZ // 2
WIDE = SIDE + 2 * PADJ
VROW = SIDE * 2
MASKED = -1.0e30
ROW_TYPES = [0, 1, 2, STRIPS - 2, STRIPS - 1]
S_BANK = [5, 5, 4]
KPAD = 96

PRIMED = 8
TURN_BANKS = [3, 4, 5, 7]
MAX_BANKS = {True: [4, 5], False: [0, 1, 2, 3, 4]}

AHEADS = 8
ADIM = P // AHEADS
GH = 4
GROUPS = AHEADS // GH
CHUNKS = -(-TOK // P)
TOKP = CHUNKS * P
LAST = TOK - (CHUNKS - 1) * P
Q_PARTS = [0, 1, 2, 0, 1, 0]
K_PARTS = [0, 0, 0, 1, 1, 2]
ROWS = len(Q_PARTS) * ADIM
ROWSM = ROWS + 3

OWN = 13

NF4 = [-1.0, -0.6961928009986877, -0.5250730514526367, -0.39491748809814453, -0.28444138169288635,
       -0.18477343022823334, -0.09105003625154495, 0.0, 0.07958029955625534, 0.16093020141124725,
       0.24611230194568634, 0.33791524171829224, 0.44070982933044434, 0.5626170039176941,
       0.7229568362236023, 1.0]
NF4_BLOCK = 16


def shape_constants():
    c = np.zeros((P, 4 * P + GH + 3), np.float32)
    p = np.arange(P)
    c[:, 0:P] = np.eye(P)
    c[:, P:2 * P] = 1.0 / P
    c[:, 2 * P:3 * P] = (p[:, None] // 4 == p[None, :] // 4) / 4.0
    c[:, 3 * P:4 * P] = p[:, None] == 32 * (p[None, :] // 32) + ADIM
    c[:, 4 * P:4 * P + GH] = (p[:, None] % 32) // NDIM == np.arange(GH)[None, :]
    c[:, 4 * P + GH] = 1e-5
    c[:, 4 * P + GH + 1] = 1.0
    return c


def window_row(strip):
    return min(max(QI * strip - KSZ // 2, 0), SIDE - WI)


def first_key(i):
    return min(max(i - KSZ // 2, 0), SIDE - KSZ)


def hybrid_block(nc, images, x, consts, qkv_wT, rpb, proj_wT, proj_b, Wq, bq, Wk, bk, Wv, bv, Wo, bo,
                 qidx, scales, WT, out):
    vT_dram = nc.dram_tensor("vT_padded", (SIDE * WIDE, P), F32, kind="Internal").ap()

    with ExitStack() as ctx:
        def sb(name, shape, dt=F32):
            return ctx.enter_context(nc.sbuf_tensor(name, shape, dt))

        def sem(name):
            return ctx.enter_context(nc.semaphore(name))

        X = sb("X", [P, TOK])
        C = sb("C", [P, consts.shape[1]])
        ident, mean_w = C[:, 0:P], C[:, P:2 * P]
        group_w, pick_sum = C[:, 2 * P:3 * P], C[:, 3 * P:4 * P]
        head_mask = C[:, 4 * P:4 * P + GH]
        eps5 = C[:, 4 * P + GH:4 * P + GH + 1]
        W_qkv = sb("W_qkv", [P, 3 * P])
        W_proj = sb("W_proj", [P, P])
        W_q, W_k, W_v = sb("W_q", [P, P]), sb("W_k", [P, P]), sb("W_v", [P, P])
        W_o = sb("W_o", [P, GROUPS, P])
        W_ffn = sb("W_ffn", [P, P])
        bias_cols = sb("bias_cols", [P, 4])
        bv_rows = sb("bv_rows", [P, P])
        nat_bias = sb("nat_bias", [P, len(ROW_TYPES), 3, KEYS])
        KP = sb("KP", [P, GROUPS, GH, TOK], BF16)
        stats = sb("stats", [P, NBLK, 6])
        gn = sb("gn", [P, 12])
        maxes = sb("maxes", [P, 2, GH * CHUNKS])
        shift = sb("shift", [P, 2, P])
        shift_parts = sb("shift_parts", [P, 3, P], BF16)
        tail = sb("tail", [P, 2, BLK])
        normed = sb("normed", [P, BLK])
        scale_blocks = sb("scale_blocks", [P, P // NF4_BLOCK])

        arena = sb("arena", [P, 32192])

        def part(at, n, dt=F32):
            v = arena[:, at:at + n]
            return v if dt == F32 else v.bitcast(dt)

        QP = part(0, 12800, BF16).rearrange("p (g h t) -> p g h t", g=GROUPS, h=GH)
        q_parts = part(12800, 4704, BF16).rearrange("p (n t) -> p n t", n=3)
        k_parts = part(17504, 4704, BF16).rearrange("p (n t) -> p n t", n=3)
        VA = part(22208, 6400).rearrange("p (c h e) -> p c h e", c=CHUNKS, h=AHEADS)
        PB = part(28608, 3584).rearrange("p (s h t) -> p s h t", s=2, h=GH)
        XN = part(28608, TOK)
        SD, SQ = part(0, TOK), part(12800, TOK)
        q_full, q_rest = part(3200, TOK), part(6400, TOK)
        k_full, k_rest = part(9600, TOK), part(0, TOK)
        Qn = part(0, TOK)
        Kn = part(3136, SIDE * WIDE)
        VTs = part(6608, 28 * P).rearrange("p (c e) -> p c e", c=28)
        QB = part(10192, 2 * UNITS * 32).rearrange("p (s u e) -> p s u e", s=2, u=UNITS)
        KS = part(11088, 2 * WI * WIDE).rearrange("p (s n) -> p s n", s=2)
        SC = part(12080, 2 * UNITS * KEYS).rearrange("p (s u k) -> p s u k", s=2, u=UNITS)
        PT = part(14320, 2 * UNITS * P).rearrange("p (s u e) -> p s u e", s=2, u=UNITS)
        VP = part(17904, 2 * UNITS * P).rearrange("p (s u e) -> p s u e", s=2, u=UNITS)
        SUMS = part(21488, 64).rearrange("p (a s n) -> p a s n", a=2, s=2)
        PVM = part(23280, BLK)
        NM = part(23728, 32).rearrange("p (s n) -> p s n", s=2)
        On = part(23760, TOK)

        W_up, codes = part(1000, P), part(1200, P, I32)

        PS = ctx.enter_context(nc.psum_tensor("PS", [P, 8, 512], F32))

        weights_in = sem("weights_in")
        paced = sem("paced")
        table_filled, table_rows_in, table_cols_in = sem("table_filled"), sem("table_rows_in"), sem("table_cols_in")
        vpad_out = sem("vpad_out")
        setup_dve, setup_pool, setup_pe = sem("setup_dve"), sem("setup_pool"), sem("setup_pe")
        x_in, y_out = sem("x_in"), sem("y_out")
        block_ready = sem("block_ready")
        freed_dve, freed_act = sem("freed_dve"), sem("freed_act")
        dve_chain = sem("dve_chain")
        pads_zero = sem("pads_zero")
        rstd_in = sem("rstd_in")
        squared = sem("squared")
        normed_in = sem("normed_in")
        gn_sd = sem("gn_sd")
        gn_cols = sem("gn_cols")
        vT_out = sem("vT_out")
        keys_strip, queries_strip = sem("keys_strip"), sem("queries_strip")
        scores_in, biased, shifted, exps = sem("scores_in"), sem("biased"), sem("shifted"), sem("exps")
        turned, turned_read = sem("turned"), sem("turned_read")
        values_in = [sem("values_in0"), sem("values_in1")]
        summed, normalised = sem("summed"), sem("normalised")
        pv_in, out_strip = sem("pv_in"), sem("out_strip")
        q_split, k_split, k_chain = sem("q_split"), sem("k_split"), sem("k_chain")
        v_ones = sem("v_ones")
        parts_in = [sem("parts_in0"), sem("parts_in1")]
        max_scores, max_read = sem("max_scores"), sem("max_read")
        max_turned, shift_split, shift_in = sem("max_turned"), sem("shift_split"), sem("shift_in")
        max_chain = sem("max_chain")
        st_ready, exp_done, pv_done = sem("st_ready"), sem("exp_done"), sem("pv_done")
        attn_read, sums_spread, attn_normed, attn_proj, x_updated = (
            sem("attn_read"), sem("sums_spread"), sem("attn_normed"), sem("attn_proj"),
            sem("x_updated"))

        GN, NQ, NK, NV, PROJ, M2, V2, AQ, AK, AV, M3, V3, FFN = range(13)
        reader = {GN: "dve", NQ: "act", NK: "dve", NV: "act", PROJ: "dve", M2: "dve", V2: "act", AQ: "act",
                  AK: "act", AV: "dve", M3: "dve", V3: "act", FFN: "dve"}
        count = {s: 2 if s == GN else NBLK for s in reader}
        ready_base = {s: sum(count[t] for t in range(s)) for s in reader}
        READY = sum(count.values())
        count[GN] = 1
        freed_base = {s: sum(count[t] for t in range(s) if reader[t] == reader[s]) for s in reader}
        FREED = {e: sum(count[t] for t in reader if reader[t] == e) for e in ("dve", "act")}
        freed = {"dve": freed_dve, "act": freed_act}

        def wait_block(eng, b, stage, j):
            eng.wait_ge(block_ready, b * READY + (ready_base[stage] + j + 1))

        def wait_freed(eng, b, stage, j):
            eng.wait_ge(freed[reader[stage]], b * FREED[reader[stage]] + (freed_base[stage] + j + 1))

        def apart(eng):
            eng.sem_inc(paced, 1)

        def blk(t, j):
            return t[:, j * BLK:(j + 1) * BLK]

        block = ctx.enter_context(nc.Block())

        @block.sync
        def _(sp):
            for s in (biased, turned_read, out_strip, pv_in, exp_done, attn_read, x_updated, max_read, pv_done):
                sp.sem_inc(s, PRIMED)
            sp.sem_inc(shift_in, 16 * PRIMED)
            def load(dst, src):
                sp.dma_start(dst, src).then_inc(weights_in, 16)

            load(C[:, :], consts)
            load(W_qkv[:, :], qkv_wT)
            load(W_proj[:, :], proj_wT)
            load(W_q[:, :], Wq)
            load(W_k[:, :], Wk)
            load(W_v[:, :], Wv)
            load(W_up, WT)
            load(codes, qidx)
            load(scale_blocks[:, :], scales.rearrange("(o n) -> o n", n=P // NF4_BLOCK))
            for n, v in enumerate((proj_b, bq, bk, bo)):
                load(bias_cols[:, n:n + 1], v.rearrange("(c o) -> c o", o=1))
            load(bv_rows[:, :], bass.AP(tensor=bv.tensor, offset=0, ap=[[0, P], [1, P]]))
            sp.wait_ge(setup_dve, 1)
            for g in range(GROUPS):
                for j in range(GH):
                    h = g * GH + j
                    load(W_o[32 * j:32 * j + ADIM, g, :], Wo[h * ADIM:(h + 1) * ADIM, :])
            stage1 = arena[:, 0:3 * 13 * WJ].rearrange("p (t r k) -> p t r k", t=3, r=13)
            sp.wait_ge(table_filled, 3)
            for t, j0 in enumerate((0, QJ, SIDE - QJ)):
                for qi in range(QI):
                    for qj in range(QJ):
                        j = j0 + qj
                        at = first_key(j) - (j0 - PADJ)
                        rx = first_key(j) - j + KSZ - 1
                        q = qi * QJ + qj
                        sp.dma_start(stage1[q:P:QI * QJ, t, :, at:at + KSZ],
                                     rpb[:, :, rx:rx + KSZ]).then_inc(table_cols_in, 16)
            sp.wait_ge(table_cols_in, 16 * 3 * QI * QJ)
            for r, s in enumerate(ROW_TYPES):
                for q in range(QI * QJ):
                    i = QI * s + q // QJ
                    at = first_key(i) - window_row(s)
                    ry = first_key(i) - i + KSZ - 1
                    sp.dma_start(nat_bias[q:P:QI * QJ, r, :, at * WJ:(at + KSZ) * WJ],
                                 stage1[q:P:QI * QJ, :, ry:ry + KSZ, :].rearrange("p t r k -> p t (r k)")
                                 ).then_inc(table_rows_in, 16)
            zeros = arena[0:SIDE, 400:400 + PADJ * P].rearrange("p (k e) -> p k e", k=PADJ)
            v_img = vT_dram.rearrange("(y x) c -> y x c", x=WIDE)
            sp.dma_start(v_img[:, 0:PADJ, :], zeros).then_inc(vpad_out, 16)
            sp.dma_start(v_img[:, PADJ + SIDE:WIDE, :], zeros).then_inc(vpad_out, 16)
            sp.wait_ge(vpad_out, 32)
            sp.wait_ge(table_rows_in, 16 * len(ROW_TYPES) * QI * QJ)

            xv = x.rearrange("b c y x -> b c (y x)")
            yv = out.rearrange("b c y x -> b c (y x)")
            def load_values(row, k):
                for ky in range(WI):
                    src = bass.AP(tensor=vT_dram.tensor, offset=(row + ky) * (WIDE * P),
                                  ap=[[P, WJ], [QJ * P, UNITS], [1, P]])
                    sp.dma_start(VP[ky * WJ:(ky + 1) * WJ, k, :, :], src).then_inc(values_in[k], 16)

            with sp.Fori(0, images) as b:
                sp.dma_start(X[:, :], xv[bass.ds(b, 1)].rearrange("b c t -> (b c) t")).then_inc(x_in, 16)
                wait_freed(sp, b, NV, NBLK - 1)
                for r in range(2):
                    src = VTs[SIDE * r:SIDE * (r + 1), :, :]
                    dst = bass.AP(tensor=vT_dram.tensor, offset=(r * WIDE + PADJ) * P,
                                  ap=[[P, SIDE], [2 * WIDE * P, 28], [1, P]])
                    sp.dma_start(dst, src).then_inc(vT_out, 16)
                sp.wait_ge(vT_out, b * 32 + 32)
                sp.wait_ge(pads_zero, b * 3 + 3)

                load_values(window_row(0), 0)
                load_values(window_row(1), 1)
                with sp.Fori(1, STRIPS // 2 - 1) as t:
                    for k in range(2):
                        sp.wait_ge(pv_in, b * STRIPS + (t * 2 + (k - 1 + PRIMED)))
                        apart(sp)
                        load_values(t * 4 + (2 * k - 3), k)
                for k in range(2):
                    s = STRIPS - 2 + k
                    sp.wait_ge(pv_in, b * STRIPS + (s - 1 + PRIMED))
                    load_values(window_row(s), k)

                sp.wait_ge(q_split, b + 1)
                sp.wait_ge(k_split, b + 1)
                for g in range(GROUPS):
                    for h in range(GH):
                        c0 = (g * GH + h) * ADIM
                        for n in range(len(Q_PARTS)):
                            sp.dma_start(QP[n * ADIM:(n + 1) * ADIM, g, h, 0:TOK],
                                         q_parts[c0:c0 + ADIM, Q_PARTS[n], :]).then_inc(parts_in[g], 16)
                            sp.dma_start(KP[n * ADIM:(n + 1) * ADIM, g, h, :],
                                         k_parts[c0:c0 + ADIM, K_PARTS[n], :]).then_inc(parts_in[g], 16)
                for g in range(GROUPS):
                    sp.wait_ge(shift_split, b * (3 * GROUPS) + (3 * g + 3))
                    for h in range(GH):
                        for n in range(3):
                            sp.dma_start(QP[ROWS + n:ROWS + n + 1, g, h, :].rearrange("p (c t) -> p c t", t=P),
                                         shift_parts[h * CHUNKS:(h + 1) * CHUNKS, n, :]).then_inc(shift_in, 16)
                for j in range(NBLK):
                    wait_freed(sp, b, FFN, j)
                    sp.dma_start(yv[bass.ds(b, 1)].rearrange("b c t -> (b c) t")[:, j * BLK:(j + 1) * BLK],
                                 blk(X, j)).then_inc(y_out, 16)
                sp.wait_ge(y_out, b * (16 * NBLK) + 16 * NBLK)
                apart(sp)

        @block.gpsimd
        def _(pool):
            pool.wait_ge(weights_in, 16 * 22)
            nc.gpsimd.memset(KP[96:128, :, :, :], 1.0).then_inc(setup_pool, 1)
            pool.wait_ge(setup_pool, 1)

            with pool.Fori(0, images) as b:
                nc.gpsimd.memset(Kn, 0.0).then_inc(pads_zero, 1)
                pool.wait_ge(pads_zero, b * 3 + 1)
                apart(pool)
                nc.gpsimd.memset(PT[64:96, :, :, :], 0.0).then_inc(pads_zero, 1)
                nc.gpsimd.memset(VP[64:96, :, :, :], 0.0).then_inc(pads_zero, 1)
                pool.wait_ge(pads_zero, b * 3 + 3)
                apart(pool)

                def spread_queries(tok0, k):
                    for i in range(QI):
                        src = Qn[:, bass.ds(tok0 + i * SIDE, SIDE)] if not isinstance(tok0, int) else \
                            Qn[:, tok0 + i * SIDE:tok0 + (i + 1) * SIDE]
                        dst = QB[:, k, :, :].rearrange("p u (h i j) -> p u h i j", h=GH, i=QI)[:, :, :, i, :]
                        src = src.rearrange("p (u o j) -> p u o j", o=1, j=QJ).to_broadcast([P, UNITS, GH, QJ])
                        m = head_mask.rearrange("p (o h a) -> p o h a", o=1, a=1).to_broadcast([P, UNITS, GH, QJ])
                        nc.gpsimd.tensor_tensor(dst, src, m, ALU.mult).then_inc(queries_strip, 1)

                def subtract_max(n, k):
                    pool.wait_ge(biased, (n + 1) * 6 + PRIMED)
                    m = NM[:, k, 0:UNITS].rearrange("p (u o) -> p u o", o=1).to_broadcast([P, UNITS, KEYS])
                    nc.gpsimd.tensor_tensor(SC[:, k, :, :], SC[:, k, :, :], m, ALU.add).then_inc(shifted, 1)

                def normalise(n, k):
                    pool.wait_ge(summed, n * 2 + 2)
                    r = SUMS[:, 1, k, 0:UNITS].rearrange("p (u o) -> p u o", o=1).to_broadcast([P, UNITS, KEYS])
                    nc.gpsimd.tensor_tensor(SC[:, k, :, :], SC[:, k, :, :], r, ALU.mult).then_inc(normalised, 1)

                wait_freed(pool, b, NQ, NBLK - 1)
                apart(pool)
                base = b * STRIPS

                def queries(s, k):
                    if not (isinstance(s, int) and s < 2):
                        pool.wait_ge(scores_in, base + (s - 1))
                    spread_queries(s * (QI * SIDE), k)

                queries(0, 0)
                queries(1, 1)
                with pool.Fori(0, STRIPS // 2 - 1) as t:
                    for k in range(2):
                        subtract_max(base + (t * 2 + k), k)
                        queries(t * 2 + (k + 2), k)
                        normalise(base + (t * 2 + k), k)
                for k in range(2):
                    subtract_max(base + (STRIPS - 2 + k), k)
                    normalise(base + (STRIPS - 2 + k), k)

                wait_freed(pool, b, AK, NBLK - 1)
                apart(pool)
                chain = [0]

                def own(ins):
                    ins.then_inc(k_chain, 1)
                    chain[0] += 1
                    pool.wait_ge(k_chain, b * 3 + chain[0])
                    apart(pool)

                own(nc.gpsimd.tensor_copy(k_parts[:, 0, :], k_full))
                own(nc.gpsimd.tensor_tensor(k_rest, k_full, k_parts[:, 0, :], ALU.subtract))
                own(nc.gpsimd.tensor_copy(k_parts[:, 1, :], k_rest))
                nc.gpsimd.tensor_tensor(k_parts[:, 2, :], k_rest, k_parts[:, 1, :],
                                        ALU.subtract).then_inc(k_split, 1)
                nc.gpsimd.memset(VA[:, 0:CHUNKS - 1, :, ADIM:32], 1.0).then_inc(v_ones, 1)
                nc.gpsimd.memset(VA[0:LAST, CHUNKS - 1, :, ADIM:32], 1.0).then_inc(v_ones, 1)
                pool.wait_ge(v_ones, b * 3 + 2)
                apart(pool)
                nc.gpsimd.memset(VA[LAST:P, CHUNKS - 1, :, :], 0.0).then_inc(v_ones, 1)
                pool.wait_ge(v_ones, b * 3 + 3)
                wait_freed(pool, b, FFN, NBLK - 1)

        @block.tensor
        def _(pe):
            mm = nc.tensor.matmul

            pe.wait_ge(setup_dve, len(NF4) + 3)
            pe.wait_ge(weights_in, 16 * 22)
            pe.wait_ge(setup_pool, 1)
            mm(PS[:, 0, 0:P], normed[:, 0:P], W_up, start=True, stop=True).then_inc(setup_pe, 1)
            pe.wait_ge(setup_dve, len(NF4) + 4)

            with pe.Fori(0, images) as b:
                for n in range(2):
                    pe.wait_ge(gn_cols, b * 3 + (n + 1))
                    mm(PS[:, 7, n:n + 1], group_w, gn[:, 3 * n:3 * n + 1], start=True,
                       stop=True).then_inc(block_ready, 1)
                pe.wait_ge(gn_cols, b * 3 + 3)
                for j in range(NBLK):
                    mm(PS[:, j, 0:BLK], W_qkv[:, 0:P], blk(XN, j), start=True, stop=True).then_inc(block_ready, 1)
                for j in range(NBLK):
                    wait_freed(pe, b, NQ, j)
                    mm(PS[:, j, 0:BLK], W_qkv[:, P:2 * P], blk(XN, j), start=True, stop=True).then_inc(block_ready, 1)
                for j in range(NBLK):
                    wait_freed(pe, b, NK, j)
                    for c in range(4):
                        t0 = (4 * j + c) * VROW
                        m = mm(PS[0:VROW, j, c * P:(c + 1) * P], XN[:, t0:t0 + VROW], W_qkv[:, 2 * P:3 * P],
                               start=True, stop=True)
                    m.then_inc(block_ready, 1)
                wait_freed(pe, b, NV, NBLK - 1)
                pe.wait_ge(pads_zero, b * 3 + 3)

                base = b * STRIPS
                s_at = [(0, u) if u < 5 else (1, u - 5) if u < 10 else (2, u - 10) for u in range(UNITS)]

                def scores(n, k):
                    pe.wait_ge(keys_strip, n + 1)
                    pe.wait_ge(queries_strip, n * 2 + 2)
                    pe.wait_ge(biased, n * 6 + (PRIMED - 1))
                    apart(pe)
                    win = KS[:, k, :].rearrange("p (y x) -> p y x", x=WIDE)
                    for u in range(UNITS):
                        bk_, at = s_at[u]
                        for g in range(4):
                            r = slice(32 * g, 32 * g + 32)
                            m = mm(PS[r, bk_, at * KEYS:(at + 1) * KEYS], QB[r, k, u, :],
                                   win[r, :, u * QJ:u * QJ + WJ], start=True, stop=True,
                                   tile_position=(32 * g, 32 * g))
                    m.then_inc(scores_in, 1)

                def turn(n, k):
                    pe.wait_ge(normalised, n + 1)
                    for c in range(4):
                        pe.wait_ge(turned_read, n * 4 + (c - 3 + PRIMED))
                        for u in range(4 * c, min(4 * c + 4, UNITS)):
                            m = nc.tensor.transpose(PS[0:KEYS, TURN_BANKS[c], (u % 4) * P:(u % 4 + 1) * P],
                                                    SC[:, k, u, :], ident)
                        m.then_inc(turned, 1)

                def values(n, k, visit):
                    pe.wait_ge(turned_read, n * 4 + (4 + PRIMED))
                    pe.wait_ge(out_strip, n * 3 + PRIMED)
                    pe.wait_ge(values_in[k], visit)
                    for u in range(UNITS):
                        for g in range(4):
                            m = mm(PS[32 * g:32 * g + 32, 6, 32 * u:32 * u + 32],
                                   VP[0:KPAD, k, u, 32 * g:32 * g + 32], PT[0:KPAD, k, u, 32 * g:32 * g + 32],
                                   start=True, stop=True, tile_position=(0, 32 * g))
                    m.then_inc(pv_in, 1)

                VIS = 16 * WI
                per = STRIPS // 2 * VIS
                scores(base, 0)
                scores(base + 1, 1)
                turn(base, 0)
                with pe.Fori(1, STRIPS // 2) as t:
                    scores(base + t * 2, 0)
                    values(base + (t * 2 - 2), 0, b * per + t * VIS)
                    turn(base + (t * 2 - 1), 1)
                    scores(base + (t * 2 + 1), 1)
                    values(base + (t * 2 - 1), 1, b * per + t * VIS)
                    turn(base + t * 2, 0)
                values(base + (STRIPS - 2), 0, b * per + per)
                turn(base + (STRIPS - 1), 1)
                values(base + (STRIPS - 1), 1, b * per + per)
                pe.wait_ge(out_strip, b * (3 * STRIPS) + 3 * STRIPS + PRIMED)

                for j in range(NBLK):
                    mm(PS[:, j, 0:BLK], W_proj[:, :], blk(On, j), start=True, stop=True).then_inc(block_ready, 1)

                def layer_norm(mean_stage, var_stage, before, visit):
                    for j in range(NBLK):
                        wait_freed(pe, b, before, j) if before is not None else None
                        mm(PS[:, j, 0:BLK], mean_w, blk(X, j), start=True, stop=True).then_inc(block_ready, 1)
                    for j in range(NBLK):
                        wait_freed(pe, b, mean_stage, j)
                        pe.wait_ge(squared, b * (2 * NBLK) + (visit * NBLK + j + 1))
                        mm(PS[:, j, 0:BLK], mean_w, blk(SQ, j), start=True, stop=True).then_inc(block_ready, 1)

                layer_norm(M2, V2, PROJ, 0)
                for j in range(NBLK):
                    wait_freed(pe, b, V2, j)
                    pe.wait_ge(normed_in, b * (2 * NBLK) + (j + 1))
                    mm(PS[:, j, 0:BLK], W_q[:, :], blk(XN, j), start=True, stop=True).then_inc(block_ready, 1)
                for j in range(NBLK):
                    wait_freed(pe, b, AQ, j)
                    mm(PS[:, j, 0:BLK], W_k[:, :], blk(XN, j), start=True, stop=True).then_inc(block_ready, 1)
                for j in range(NBLK):
                    wait_freed(pe, b, AK, j)
                    for c in range(4 * j, min(4 * j + 4, CHUNKS)):
                        n = LAST if c == CHUNKS - 1 else P
                        m = mm(PS[0:n, j, (c % 4) * P:(c % 4 + 1) * P], XN[:, c * P:c * P + n], W_v[:, :],
                               start=True, stop=True)
                    m.then_inc(block_ready, 1)
                wait_freed(pe, b, AV, NBLK - 1)

                def attention(exp_g, max_g):
                    if exp_g is not None:
                        pe.wait_ge(shift_in, b * (GROUPS * 16 * 3 * GH) + (exp_g + 1) * 16 * 3 * GH + 16 * PRIMED)
                        pe.wait_ge(v_ones, b * 3 + 3)
                    if max_g is not None:
                        pe.wait_ge(parts_in[max_g], b * (16 * 2 * GH * len(Q_PARTS)) + 16 * 2 * GH * len(Q_PARTS))
                    apart(pe)
                    banks = MAX_BANKS[exp_g is not None]

                    def spread(e):
                        pe.wait_ge(attn_read, e + (1 + PRIMED))
                        pe.wait_ge(x_updated, e + PRIMED)
                        mm(PS[:, 7, 0:BLK], pick_sum, tail[:, 0, :], start=True, stop=True).then_inc(sums_spread, 1)

                    def project(e):
                        pe.wait_ge(attn_normed, e * 2 + 2)
                        mm(PS[:, 7, 0:BLK], W_o[:, exp_g, :], normed[:, :], start=True,
                           stop=True).then_inc(attn_proj, 1)

                    def key_block(i, first):
                        e = b * (GROUPS * NBLK) + (i + exp_g * NBLK) if exp_g is not None else None
                        mi = b * (GROUPS * NBLK) + (i + max_g * NBLK) if max_g is not None else None
                        at = slice(i * BLK, (i + 1) * BLK) if isinstance(i, int) else bass.ds(i * BLK, BLK)

                        def weigh(c):
                            pe.wait_ge(exp_done, e * (2 * CHUNKS) + (2 * c + 2 + PRIMED))
                            if c == 0:
                                pe.wait_ge(attn_read, e + PRIMED)
                            for h in range(GH):
                                m = mm(PS[32 * h:32 * h + 32, 6, 0:BLK], VA[:, c, exp_g * GH + h, :],
                                       PB[:, c % 2, h, :], start=(c == 0), stop=(c == CHUNKS - 1),
                                       tile_position=(0, 32 * h))
                            m.then_inc(pv_done, 1)

                        def scores_turned(c, p, n):
                            pe.wait_ge(exp_done, e * (2 * CHUNKS) + (2 * c + p - 1 + PRIMED))
                            if n < P:
                                apart(pe)
                            for h in (2 * p, 2 * p + 1):
                                m = mm(PS[0:n, h, 0:BLK], KP[0:ROWSM, exp_g, h, c * P:c * P + n],
                                       QP[0:ROWSM, exp_g, h, at], start=True, stop=True)
                            m.then_inc(st_ready, 1)

                        def scores_for_max(c, h, n):
                            u = c * GH + h
                            pe.wait_ge(max_read, mi * (CHUNKS * GH) + (u + 1 - len(banks) + PRIMED))
                            if n < P:
                                apart(pe)
                            mm(PS[0:n, banks[u % len(banks)], 0:BLK], QP[0:ROWS, max_g, h, c * P:c * P + n],
                               KP[0:ROWS, max_g, h, at], start=True, stop=True).then_inc(max_scores, 1)

                        for c in range(CHUNKS):
                            n = LAST if c == CHUNKS - 1 else P
                            if max_g is not None:
                                scores_for_max(c, 0, n)
                            if exp_g is not None:
                                scores_turned(c, 0, n)
                            if max_g is not None:
                                scores_for_max(c, 1, n)
                            if exp_g is not None:
                                scores_turned(c, 1, n)
                            if max_g is not None:
                                scores_for_max(c, 2, n)
                            if exp_g is not None and c > 0:
                                weigh(c - 1)
                            if max_g is not None:
                                scores_for_max(c, 3, n)
                            if exp_g is not None and not first and c == 2:
                                spread(e - 1)
                            if exp_g is not None and not first and c == 6:
                                project(e - 1)
                        if exp_g is not None:
                            weigh(CHUNKS - 1)

                    key_block(0, True)
                    with pe.Fori(1, NBLK) as i:
                        key_block(i, False)
                    if exp_g is not None:
                        last = b * (GROUPS * NBLK) + ((exp_g + 1) * NBLK - 1)
                        spread(last)
                        project(last)
                        pe.wait_ge(x_updated, b * (GROUPS * NBLK) + ((exp_g + 1) * NBLK + PRIMED))
                    if max_g is not None:
                        pe.wait_ge(max_chain, b * (GROUPS * NBLK) + (max_g + 1) * NBLK)
                        nc.tensor.transpose(PS[0:GH * CHUNKS, 7, 0:P], maxes[:, 1, :], ident).then_inc(max_turned, 1)
                        pe.wait_ge(shift_split, b * (3 * GROUPS) + (3 * max_g + 1))

                attention(None, 0)
                attention(0, 1)
                attention(1, None)

                layer_norm(M3, V3, None, 1)
                for j in range(NBLK):
                    wait_freed(pe, b, V3, j)
                    pe.wait_ge(normed_in, b * (2 * NBLK) + (NBLK + j + 1))
                    mm(PS[:, j, 0:BLK], W_ffn[:, :], blk(XN, j), start=True, stop=True).then_inc(block_ready, 1)
                wait_freed(pe, b, FFN, NBLK - 1)

        @block.scalar
        def _(act):
            act.wait_ge(weights_in, 16 * 22)
            with act.Fori(0, images) as b:
                wait_block(act, b, GN, 1)
                nc.scalar.activation(gn[:, 7:8], PS[:, 7, 1:2], ACT.Sqrt, bias=eps5).then_inc(gn_sd, 1)
                for j in range(NBLK):
                    wait_block(act, b, NQ, j)
                    nc.scalar.activation(blk(Qn, j), PS[:, j, 0:BLK], ACT.Copy,
                                         scale=float(NDIM) ** -0.5).then_inc(freed_act, 1)
                for j in range(NBLK):
                    wait_block(act, b, NV, j)
                    nc.scalar.activation(VTs[0:VROW, 4 * j:4 * j + 4, :].rearrange("p c e -> p (c e)"),
                                         PS[0:VROW, j, :], ACT.Copy).then_inc(freed_act, 1)

                base = b * STRIPS
                wait_freed(act, b, NK, NBLK - 1)
                act.wait_ge(pads_zero, b * 3 + 3)

                def keys(n, row, k, first):
                    if not first:
                        act.wait_ge(scores_in, n - 1)
                    src = Kn[:, bass.ds(row * WIDE, WI * WIDE)] if not isinstance(row, int) else \
                        Kn[:, row * WIDE:(row + WI) * WIDE]
                    nc.scalar.activation(KS[:, k, :], src, ACT.Copy).then_inc(keys_strip, 1)

                def exponentials(n, k):
                    act.wait_ge(shifted, n + 1)
                    v = SC[:, k, :, :].rearrange("p u k -> p (u k)")
                    nc.scalar.activation(v, v, ACT.Exp).then_inc(exps, 1)

                def read_turned(n, k):
                    for c in range(4):
                        act.wait_ge(turned, n * 4 + (c + 1))
                        if c == 0:
                            act.wait_ge(pv_in, n + (PRIMED - 1))
                        u0, u1 = 4 * c, min(4 * c + 4, UNITS)
                        nc.scalar.activation(PT[0:KEYS, k, u0:u1, :].rearrange("p u e -> p (u e)"),
                                             PS[0:KEYS, TURN_BANKS[c], 0:(u1 - u0) * P], ACT.Copy).then_inc(turned_read, 1)

                keys(base, window_row(0), 0, True)
                keys(base + 1, window_row(1), 1, True)
                exponentials(base, 0)
                keys(base + 2, window_row(2), 0, False)
                with act.Fori(1, STRIPS // 2 - 2) as t:
                    read_turned(base + (t * 2 - 2), 0)
                    exponentials(base + (t * 2 - 1), 1)
                    keys(base + (t * 2 + 1), t * 4 - 1, 1, False)
                    read_turned(base + (t * 2 - 1), 1)
                    exponentials(base + t * 2, 0)
                    keys(base + (t * 2 + 2), t * 4 + 1, 0, False)
                for s in range(STRIPS - 5, STRIPS):
                    read_turned(base + (s - 1), (s - 1) % 2)
                    exponentials(base + s, s % 2)
                    if s + 2 < STRIPS:
                        keys(base + (s + 2), window_row(s + 2), s % 2, False)
                read_turned(base + (STRIPS - 1), 1)

                def layer_norm(mean_stage, var_stage):
                    for j in range(NBLK):
                        wait_freed(act, b, mean_stage, j)
                        nc.scalar.activation(blk(SQ, j), blk(XN, j), ACT.Square).then_inc(squared, 1)
                    for j in range(NBLK):
                        wait_block(act, b, var_stage, j)
                        nc.scalar.activation(blk(SD, j), PS[:, j, 0:BLK], ACT.Ln, bias=eps5).then_inc(freed_act, 1)
                    for j in range(NBLK):
                        if j == 0:
                            wait_freed(act, b, var_stage, NBLK - 1)
                        nc.scalar.activation(blk(SD, j), blk(SD, j), ACT.Exp, scale=-0.5).then_inc(rstd_in, 1)

                layer_norm(M2, V2)
                for stage, full, col in ((AQ, q_full, 1), (AK, k_full, 2)):
                    for j in range(NBLK):
                        wait_block(act, b, stage, j)
                        ins = nc.scalar.activation(blk(full, j), PS[:, j, 0:BLK], ACT.Identity,
                                                   bias=bias_cols[:, col:col + 1])
                        ins.then_inc(freed_act, 1)

                def exps_of(g):
                    with act.Fori(0, NBLK) as i:
                        e = b * (GROUPS * NBLK) + (i + g * NBLK)
                        for c in range(CHUNKS):
                            n = LAST if c == CHUNKS - 1 else P
                            for p in range(2):
                                act.wait_ge(st_ready, e * (2 * CHUNKS) + (2 * c + p + 1))
                                if p == 0:
                                    act.wait_ge(pv_done, e * CHUNKS + (c - 1 + PRIMED if c else PRIMED))
                                nc.scalar.activation(PB[0:n, c % 2, 2 * p:2 * p + 2, :], PS[0:n, 2 * p:2 * p + 2, 0:BLK],
                                                     ACT.Exp, scale=float(ADIM) ** -0.5).then_inc(exp_done, 1)

                exps_of(0)
                exps_of(1)
                layer_norm(M3, V3)

        @block.vector
        def _(dve):
            V = nc.vector
            V.memset(W_o[:, :, :], 0.0).then_inc(setup_dve, 1)
            V.memset(nat_bias[:, :, :, :], MASKED).then_inc(table_filled, 1)
            V.memset(arena[:, 0:3 * 13 * WJ], MASKED).then_inc(table_filled, 1)
            V.memset(arena[:, 400:800], 0.0).then_inc(table_filled, 1)
            V.memset(maxes[:, 0, :], 0.0).then_inc(setup_dve, 1)
            dve.wait_ge(weights_in, 16 * 22)
            w, term = normed[:, 0:P], tail[:, 0, 0:P]
            for k, value in enumerate(NF4):
                V.tensor_scalar(term, codes, float(k), value, ALU.is_equal, ALU.mult).then_inc(dve_chain, 1)
                dve.wait_ge(dve_chain, k + 1)
                if k == 0:
                    V.tensor_copy(w, term).then_inc(setup_dve, 1)
                else:
                    V.tensor_tensor(w, w, term, ALU.add).then_inc(setup_dve, 1)
                dve.wait_ge(setup_dve, k + 3)
            wv = w.rearrange("p (n e) -> p n e", e=NF4_BLOCK)
            s = scale_blocks[:, :].rearrange("p (n o) -> p n o", o=1).to_broadcast([P, P // NF4_BLOCK, NF4_BLOCK])
            V.tensor_tensor(wv, wv, s, ALU.mult).then_inc(setup_dve, 1)
            dve.wait_ge(setup_pe, 1)
            V.tensor_copy(W_ffn[:, :], PS[:, 0, 0:P]).then_inc(setup_dve, 1)
            dve.wait_ge(table_rows_in, 16 * len(ROW_TYPES) * QI * QJ)
            dve.wait_ge(vpad_out, 32)

            with dve.Fori(0, images) as b:
                chain = [0]

                def own(ins, alone=False):
                    ins.then_inc(dve_chain, 1)
                    chain[0] += 1
                    dve.wait_ge(dve_chain, b * OWN + (len(NF4) + chain[0]))
                    if alone:
                        apart(dve)

                dve.wait_ge(x_in, b * 16 + 16)
                for j in range(NBLK):
                    ins = V.bn_stats(stats[:, j, :], blk(X, j))
                own(ins, alone=True)
                V.bn_aggr(gn[:, 0:2], stats[:, :, :]).then_inc(gn_cols, 1)
                wait_block(dve, b, GN, 0)
                V.tensor_copy(gn[:, 4:5], PS[:, 7, 0:1]).then_inc(freed_dve, 1)
                wait_freed(dve, b, GN, 0)
                own(V.tensor_tensor(gn[:, 5:6], gn[:, 0:1], gn[:, 4:5], ALU.subtract))
                own(V.tensor_tensor(gn[:, 6:7], gn[:, 5:6], gn[:, 5:6], ALU.mult))
                V.tensor_tensor(gn[:, 3:4], gn[:, 6:7], gn[:, 1:2], ALU.add).then_inc(gn_cols, 1)
                dve.wait_ge(gn_sd, b + 1)
                own(V.reciprocal(gn[:, 8:9], gn[:, 7:8]))
                V.tensor_scalar(XN, X[:, :], gn[:, 4:5], gn[:, 8:9], ALU.subtract, ALU.mult).then_inc(gn_cols, 1)
                dve.wait_ge(pads_zero, b * 3 + 3)
                k_img = Kn.rearrange("p (y x) -> p y x", x=WIDE)
                rows = BLK // SIDE
                for j in range(NBLK):
                    wait_block(dve, b, NK, j)
                    V.tensor_copy(k_img[:, rows * j:rows * (j + 1), PADJ:PADJ + SIDE],
                                  PS[:, j, 0:BLK].rearrange("p (y x) -> p y x", x=SIDE)).then_inc(freed_dve, 1)

                base = b * STRIPS

                def add_bias(n, k, row_type, first):
                    dve.wait_ge(scores_in, n + 1)
                    if not first:
                        dve.wait_ge(turned, (n - 1) * 4)
                    for bk_, u0, u1, kind in ((0, 0, 1, 0), (0, 1, 5, 1), (1, 5, 10, 1), (2, 10, 13, 1), (2, 13, 14, 2)):
                        at = (u0 - (0, 5, 10)[bk_]) * KEYS
                        m = u1 - u0
                        V.tensor_tensor(
                            SC[:, k, u0:u1, :], PS[:, bk_, at:at + m * KEYS].rearrange("p (u k) -> p u k", u=m),
                            nat_bias[:, row_type, kind:kind + 1, :].to_broadcast([P, m, KEYS]),
                            ALU.add).then_inc(biased, 1)
                    dve.wait_ge(biased, n * 6 + 5 + PRIMED)
                    V.tensor_reduce(NM[:, k, 0:UNITS], SC[:, k, :, :], AX.X, ALU.max, negate=True).then_inc(biased, 1)

                def sum_up(n, k):
                    dve.wait_ge(exps, n + 1)
                    V.tensor_reduce(SUMS[:, 0, k, 0:UNITS], SC[:, k, :, :], AX.X, ALU.add).then_inc(summed, 1)
                    dve.wait_ge(summed, n * 2 + 1)
                    V.reciprocal(SUMS[:, 1, k, 0:UNITS], SUMS[:, 0, k, 0:UNITS]).then_inc(summed, 1)

                def finish(n, k, tok0):
                    dve.wait_ge(pv_in, n + (1 + PRIMED))
                    V.tensor_tensor(PVM.rearrange("p (u h q) -> p u h q", u=UNITS, h=GH),
                                    PS[:, 6, 0:BLK].rearrange("p (u h q) -> p u h q", u=UNITS, h=GH),
                                    head_mask.rearrange("p (o h a) -> p o h a", o=1, a=1)
                                    .to_broadcast([P, UNITS, GH, QI * QJ]), ALU.mult).then_inc(out_strip, 1)
                    dve.wait_ge(out_strip, n * 3 + (1 + PRIMED))
                    v = PVM.rearrange("p (u h i j) -> p i u j h", u=UNITS, h=GH, i=QI)
                    for i in range(QI):
                        o = On[:, tok0 + i * SIDE:tok0 + (i + 1) * SIDE] if isinstance(tok0, int) else \
                            On[:, bass.ds(tok0 + i * SIDE, SIDE)]
                        V.tensor_reduce(o.rearrange("p (u j) -> p u j", u=UNITS), v[:, i], AX.X,
                                        ALU.add).then_inc(out_strip, 1)

                ROW = QI * SIDE
                add_bias(base, 0, 0, True)
                sum_up(base, 0)
                add_bias(base + 1, 1, 1, True)
                sum_up(base + 1, 1)
                with dve.Fori(1, STRIPS // 2 - 1) as t:
                    for k in range(2):
                        add_bias(base + (t * 2 + k), k, 2, False)
                        finish(base + (t * 2 + (k - 2)), k, t * (2 * ROW) + (k - 2) * ROW)
                        sum_up(base + (t * 2 + k), k)
                for s in (STRIPS - 2, STRIPS - 1):
                    add_bias(base + s, s % 2, s - (STRIPS - 5), False)
                    finish(base + (s - 2), s % 2, (s - 2) * ROW)
                    sum_up(base + s, s % 2)
                finish(base + (STRIPS - 2), 0, (STRIPS - 2) * ROW)
                finish(base + (STRIPS - 1), 1, (STRIPS - 1) * ROW)

                for j in range(NBLK):
                    wait_block(dve, b, PROJ, j)
                    V.scalar_tensor_tensor(out=blk(X, j), in0=PS[:, j, 0:BLK], scalar=bias_cols[:, 0:1],
                                           in1=blk(X, j), op0=ALU.add, op1=ALU.add).then_inc(freed_dve, 1)

                def layer_norm(mean_stage, var_stage, visit):
                    for j in range(NBLK):
                        wait_block(dve, b, mean_stage, j)
                        V.tensor_tensor(blk(XN, j), blk(X, j), PS[:, j, 0:BLK], ALU.subtract).then_inc(freed_dve, 1)
                    for j in range(NBLK):
                        dve.wait_ge(rstd_in, b * (2 * NBLK) + (visit * NBLK + j + 1))
                        V.tensor_tensor(blk(XN, j), blk(XN, j), blk(SD, j), ALU.mult).then_inc(normed_in, 1)

                layer_norm(M2, V2, 0)
                wait_freed(dve, b, AQ, NBLK - 1)
                own(V.tensor_copy(q_parts[:, 0, :], q_full))
                own(V.tensor_tensor(q_rest, q_full, q_parts[:, 0, :], ALU.subtract))
                own(V.tensor_copy(q_parts[:, 1, :], q_rest))
                V.tensor_tensor(q_parts[:, 2, :], q_rest, q_parts[:, 1, :], ALU.subtract).then_inc(q_split, 1)
                for j in range(NBLK):
                    wait_block(dve, b, AV, j)
                    m = min(4, CHUNKS - 4 * j)
                    n = LAST if m == 1 else P
                    V.tensor_tensor(VA[0:n, 4 * j:4 * j + m, :, 0:ADIM],
                                    PS[0:n, j, 0:m * P].rearrange("p (c h e) -> p c h e", c=m, h=AHEADS),
                                    bv_rows[0:n, :].rearrange("p (o h e) -> p o h e", o=1, h=AHEADS)
                                    .to_broadcast([n, m, AHEADS, ADIM]), ALU.add).then_inc(freed_dve, 1)

                def attention(exp_g, max_g):
                    if max_g is not None:
                        own(V.memset(maxes[:, 1, :], -3.0e38), alone=True)
                    apart(dve)
                    banks = MAX_BANKS[exp_g is not None]

                    def normalise_block(e):
                        dve.wait_ge(sums_spread, e + 1)
                        V.reciprocal(tail[:, 1, :], PS[:, 7, 0:BLK]).then_inc(attn_normed, 1)
                        dve.wait_ge(attn_normed, e * 2 + 1)
                        V.tensor_tensor(normed[:, :], tail[:, 0, :], tail[:, 1, :], ALU.mult).then_inc(attn_normed, 1)

                    def update_x(e, at):
                        dve.wait_ge(attn_proj, e + 1)
                        xb = X[:, at]
                        if exp_g == 0:
                            ins = V.scalar_tensor_tensor(out=xb, in0=PS[:, 7, 0:BLK], scalar=bias_cols[:, 3:4],
                                                         in1=xb, op0=ALU.add, op1=ALU.add)
                        else:
                            ins = V.tensor_tensor(xb, xb, PS[:, 7, 0:BLK], ALU.add)
                        ins.then_inc(x_updated, 1)

                    def key_block(i, first):
                        e = b * (GROUPS * NBLK) + (i + exp_g * NBLK) if exp_g is not None else None
                        mi = b * (GROUPS * NBLK) + (i + max_g * NBLK) if max_g is not None else None
                        for c in range(CHUNKS):
                            n = LAST if c == CHUNKS - 1 else P
                            if exp_g is not None and not first and c == 4:
                                normalise_block(e - 1)
                            if exp_g is not None and not first and c == 8:
                                update_x(e - 1, bass.ds(i * BLK - BLK, BLK))
                            for h in range(GH) if max_g is not None else ():
                                u = c * GH + h
                                dve.wait_ge(max_scores, mi * (CHUNKS * GH) + (u + 1))
                                at = h * CHUNKS + c
                                V.tensor_reduce(maxes[0:n, 0, at:at + 1], PS[0:n, banks[u % len(banks)], 0:BLK],
                                                AX.X, ALU.max).then_inc(max_read, 1)
                        if exp_g is not None:
                            dve.wait_ge(pv_done, e * CHUNKS + (CHUNKS + PRIMED))
                            V.tensor_copy(tail[:, 0, :], PS[:, 6, 0:BLK]).then_inc(attn_read, 1)
                            dve.wait_ge(attn_read, e + (1 + PRIMED))
                            if max_g is None:
                                apart(dve)
                        if max_g is not None:
                            dve.wait_ge(max_read, mi * (CHUNKS * GH) + (CHUNKS * GH + PRIMED))
                            V.tensor_tensor(maxes[:, 1, :], maxes[:, 1, :], maxes[:, 0, :],
                                            ALU.max).then_inc(max_chain, 1)
                            dve.wait_ge(max_chain, mi + 1)
                            apart(dve)

                    key_block(0, True)
                    with dve.Fori(1, NBLK) as i:
                        key_block(i, False)
                    if exp_g is not None:
                        last = b * (GROUPS * NBLK) + ((exp_g + 1) * NBLK - 1)
                        normalise_block(last)
                        update_x(last, slice(TOK - BLK, TOK))
                        dve.wait_ge(x_updated, b * (GROUPS * NBLK) + ((exp_g + 1) * NBLK + PRIMED))
                    if max_g is not None:
                        rows = GH * CHUNKS
                        done = b * GROUPS + max_g
                        dve.wait_ge(max_turned, done + 1)
                        dve.wait_ge(shift_in, done * (16 * 3 * GH) + 16 * PRIMED)
                        own(V.tensor_scalar(shift[0:rows, 0, :], PS[0:rows, 7, 0:P], -1.0, None, ALU.mult))
                        V.tensor_copy(shift_parts[0:rows, 0, :], shift[0:rows, 0, :]).then_inc(shift_split, 1)
                        dve.wait_ge(shift_split, done * 3 + 1)
                        own(V.tensor_tensor(shift[0:rows, 1, :], shift[0:rows, 0, :], shift_parts[0:rows, 0, :],
                                            ALU.subtract))
                        V.tensor_copy(shift_parts[0:rows, 1, :], shift[0:rows, 1, :]).then_inc(shift_split, 1)
                        dve.wait_ge(shift_split, done * 3 + 2)
                        V.tensor_tensor(shift_parts[0:rows, 2, :], shift[0:rows, 1, :], shift_parts[0:rows, 1, :],
                                        ALU.subtract).then_inc(shift_split, 1)

                attention(None, 0)
                attention(0, 1)
                attention(1, None)

                layer_norm(M3, V3, 1)
                for j in range(NBLK):
                    wait_block(dve, b, FFN, j)
                    V.tensor_tensor(blk(X, j), blk(X, j), PS[:, j, 0:BLK], ALU.add).then_inc(freed_dve, 1)
                assert chain[0] == OWN, chain


def kernel(x, L0_conv_qkv_w, L0_conv_rpb, L0_conv_proj_w, L0_conv_proj_b, L1_attn_Wq, L1_attn_bq, L1_attn_Wk,
           L1_attn_bk, L1_attn_Wv, L1_attn_bv, L1_attn_Wo, L1_attn_bo, L1_ffn_qidx, L1_ffn_scales, L1_ffn_W):
    import concourse.bacc as bacc
    from concourse.bass_utils import run_bass_kernel_spmd

    args = {
        "x": x, "consts": shape_constants(), "qkv_wT": np.asarray(L0_conv_qkv_w).T, "rpb": L0_conv_rpb,
        "proj_wT": np.asarray(L0_conv_proj_w).T, "proj_b": L0_conv_proj_b, "Wq": L1_attn_Wq, "bq": L1_attn_bq,
        "Wk": L1_attn_Wk, "bk": L1_attn_bk, "Wv": L1_attn_Wv, "bv": L1_attn_bv, "Wo": L1_attn_Wo,
        "bo": L1_attn_bo, "qidx": L1_ffn_qidx, "scales": L1_ffn_scales, "WT": np.asarray(L1_ffn_W).T,
    }
    nc = bacc.Bacc("TRN2", target_bir_lowering=False, num_devices=1)
    arrays, aps = {}, {}
    for name, a in args.items():
        a = np.ascontiguousarray(a)
        arrays[f"in_{name}"] = a
        aps[name] = nc.dram_tensor(f"in_{name}", a.shape, mybir.dt.from_np(a.dtype), kind="ExternalInput").ap()
    aps["out"] = nc.dram_tensor("out_y", arrays["in_x"].shape, F32, kind="ExternalOutput").ap()
    hybrid_block(nc, arrays["in_x"].shape[0], **aps)
    r = run_bass_kernel_spmd(nc, [arrays], core_ids=[0])
    return r.results[0]["out_y"]
```

```python
from contextlib import ExitStack

import numpy as np

import concourse.bass as bass
from concourse import mybir

F32 = mybir.dt.float32
BF16 = mybir.dt.bfloat16
I32 = mybir.dt.int32
ALU = mybir.AluOpType
ACT = mybir.ActivationFunctionType
AX = mybir.AxisListType

P = 128
SIDE = 56
TOK = SIDE * SIDE
BLK = 448
NBLK = TOK // BLK

KSZ = 7
NHEADS = 16
NDIM = P // NHEADS
QI, QJ = 2, 4
WI, WJ = QI + KSZ - 1, QJ + KSZ - 1
KEYS = WI * WJ
UNITS = SIDE // QJ
STRIPS = SIDE // QI
PADJ = KSZ // 2
WIDE = SIDE + 2 * PADJ
VROW = SIDE * 2
MASKED = -1.0e30
ROW_TYPES = [0, 1, 2, STRIPS - 2, STRIPS - 1]
KPAD = 96

PRIMED = 8
TURN_BANKS = [3, 4, 5, 7]

AHEADS = 8
ADIM = P // AHEADS
GH = 4
GROUPS = AHEADS // GH
CHUNKS = -(-TOK // P)
LAST = TOK - (CHUNKS - 1) * P
Q_PARTS = [0, 1, 2, 0, 1, 0]
K_PARTS = [0, 0, 0, 1, 1, 2]
HIGH_ROWS = [n for n, m in enumerate(K_PARTS) if m == 0]
ROWS = len(Q_PARTS) * ADIM
ROWSM = ROWS + 3
AUNITS = GROUPS * NBLK
ST_BANKS, ALL_ST_BANKS = 3, 6
QCH = 4
QN = BLK // QCH
MAXES = QCH * GH * NBLK
SPREAD_AT, INVERT_AT, PROJECT_AT, UPDATE_AT, TAIL_DONE = 1, 2, 3, 4, 5
MAX_CHUNKS = 22


def max_steps(c):
    at = (c - MAX_CHUNKS) % CHUNKS
    return range(-(-MAXES * at // CHUNKS), -(-MAXES * (at + 1) // CHUNKS))


FIRST_STEPS = max_steps(0).start


def max_banks():
    last, steps = {}, []
    for m in range(MAXES):
        if m < max_steps(TAIL_DONE).start:
            bank = [3, 4, 5][m % 3]
        else:
            bank = [7, 3, 4, 5][(m - max_steps(TAIL_DONE).start) % 4]
        steps.append((bank, last.get(bank)))
        last[bank] = m
    return steps, last


MAX_PIECES = [(0, 2), (2, 4), (4, NBLK)]


def max_step(m):
    return m // (GH * NBLK), m // NBLK % GH, m % NBLK


OWN = 3

NF4 = [-1.0, -0.6961928009986877, -0.5250730514526367, -0.39491748809814453, -0.28444138169288635,
       -0.18477343022823334, -0.09105003625154495, 0.0, 0.07958029955625534, 0.16093020141124725,
       0.24611230194568634, 0.33791524171829224, 0.44070982933044434, 0.5626170039176941,
       0.7229568362236023, 1.0]
NF4_BLOCK = 16


def shape_constants():
    c = np.zeros((P, 4 * P + GH + 1), np.float32)
    p = np.arange(P)
    c[:, 0:P] = np.eye(P)
    c[:, P:2 * P] = 1.0 / P
    c[:, 2 * P:3 * P] = (p[:, None] // 4 == p[None, :] // 4) / 4.0
    c[:, 3 * P:4 * P] = p[:, None] == 32 * (p[None, :] // 32) + ADIM
    c[:, 4 * P:4 * P + GH] = (p[:, None] % 32) // NDIM == np.arange(GH)[None, :]
    c[:, 4 * P + GH] = 1e-5
    return c


def window_row(strip):
    return min(max(QI * strip - KSZ // 2, 0), SIDE - WI)


def first_key(i):
    return min(max(i - KSZ // 2, 0), SIDE - KSZ)


def hybrid_block(nc, images, x, consts, qkv_wT, rpb, proj_wT, proj_b, Wq, bq, Wk, bk, Wv, bv, Wo, bo,
                 qidx, scales, WT, out):
    vT_dram = nc.dram_tensor("vT_padded", (SIDE * WIDE, P), F32, kind="Internal").ap()

    with ExitStack() as ctx:
        def sb(name, shape, dt=F32):
            return ctx.enter_context(nc.sbuf_tensor(name, shape, dt))

        def sem(name):
            return ctx.enter_context(nc.semaphore(name))

        X = sb("X", [P, TOK])
        C = sb("C", [P, consts.shape[1]])
        ident, mean_w = C[:, 0:P], C[:, P:2 * P]
        group_w, pick_sum = C[:, 2 * P:3 * P], C[:, 3 * P:4 * P]
        head_mask = C[:, 4 * P:4 * P + GH]
        eps5 = C[:, 4 * P + GH:4 * P + GH + 1]
        W_qkv = sb("W_qkv", [P, 3 * P])
        W_proj = sb("W_proj", [P, P])
        W_q, W_k, W_v = sb("W_q", [P, P]), sb("W_k", [P, P]), sb("W_v", [P, P])
        W_o = sb("W_o", [P, GROUPS, P])
        W_ffn = sb("W_ffn", [P, P])
        bias_cols = sb("bias_cols", [P, 4])
        bv_rows = sb("bv_rows", [P, P])
        nat_bias = sb("nat_bias", [P, len(ROW_TYPES), 3, KEYS])
        KP = sb("KP", [P, GROUPS, GH, TOK], BF16)
        stats = sb("stats", [P, NBLK, 6])
        gn = sb("gn", [P, 12])
        block_max = sb("block_max", [P, GH * QCH, NBLK])
        row_max = sb("row_max", [P, GH * QCH])
        shift = sb("shift", [GH * QCH, 2, QN])
        shift_parts = sb("shift_parts", [GH * QCH, 3, QN], BF16)
        tail = sb("tail", [P, 2, BLK])
        normed = sb("normed", [P, BLK])
        scale_blocks = sb("scale_blocks", [P, P // NF4_BLOCK])

        arena = sb("arena", [P, 32192])

        def part(at, n, dt=F32):
            v = arena[:, at:at + n]
            return v if dt == F32 else v.bitcast(dt)

        QP = part(0, GROUPS * GH * TOK // 2, BF16).rearrange("p (g t) -> p g t", g=GROUPS)
        q_parts = part(12800, 4704, BF16).rearrange("p (n t) -> p n t", n=3)
        k_parts = part(17504, 4704, BF16).rearrange("p (n t) -> p n t", n=3)
        VA = part(22208, 6400).rearrange("p (c h e) -> p c h e", c=CHUNKS, h=AHEADS)
        PB = [part(at, GH * BLK).rearrange("p (h t) -> p h t", h=GH) for at in (28608, 30400, 15936)]
        XN = part(28608, TOK)
        XF = part(12800, TOK)
        SD, SQ = part(0, TOK), part(3200, TOK)
        q_full, q_rest = part(22208, TOK), part(25344, TOK)
        k_full, k_rest = part(6400, TOK), part(9536, TOK)
        Qn = part(0, TOK)
        Kn = part(3136, SIDE * WIDE)
        VTs = part(6608, 28 * P).rearrange("p (c e) -> p c e", c=28)
        QB = part(10192, 2 * UNITS * 32).rearrange("p (s u e) -> p s u e", s=2, u=UNITS)
        KS = part(11088, 2 * WI * WIDE).rearrange("p (s n) -> p s n", s=2)
        SC = part(15936, 2 * UNITS * KEYS).rearrange("p (s u k) -> p s u k", s=2, u=UNITS)
        PT = part(18176, 2 * UNITS * P).rearrange("p (s u e) -> p s u e", s=2, u=UNITS)
        VP = part(21760, 2 * UNITS * P).rearrange("p (s u e) -> p s u e", s=2, u=UNITS)
        On = part(25344, TOK)
        SUMS = part(12080, 64).rearrange("p (a s n) -> p a s n", a=2, s=2)
        NM = part(12144, 32).rearrange("p (s n) -> p s n", s=2)
        PVM = part(12176, BLK)

        W_up, codes = part(1000, P), part(1200, P, I32)

        by_column, zero_words = part(25344, 3 * 13 * WJ), part(25744, PADJ * P)

        PS = ctx.enter_context(nc.psum_tensor("PS", [P, 8, 512], F32))

        weights_in = sem("weights_in")
        paced = sem("paced")
        table_filled, table_rows_in, table_cols_in = sem("table_filled"), sem("table_rows_in"), sem("table_cols_in")
        vpad_out = sem("vpad_out")
        setup_dve, setup_pool, setup_pe = sem("setup_dve"), sem("setup_pool"), sem("setup_pe")
        x_in, y_out = sem("x_in"), sem("y_out")
        stats_in = sem("stats_in")
        block_ready = sem("block_ready")
        freed_dve, freed_act = sem("freed_dve"), sem("freed_act")
        dve_chain = sem("dve_chain")
        pads_zero = sem("pads_zero")
        rstd_in = sem("rstd_in")
        squared = sem("squared")
        normed_in = sem("normed_in")
        gn_log, gn_rstd = sem("gn_log"), sem("gn_rstd")
        gn_cols = sem("gn_cols")
        vT_out = sem("vT_out")
        keys_strip, queries_strip = sem("keys_strip"), sem("queries_strip")
        scores_in, biased, shifted, exps = sem("scores_in"), sem("biased"), sem("shifted"), sem("exps")
        turned, turned_read = sem("turned"), sem("turned_read")
        values_in = [sem("values_in0"), sem("values_in1")]
        summed, normalised = sem("summed"), sem("normalised")
        pv_in, out_strip = sem("pv_in"), sem("out_strip")
        q_split, k_split, k_rest_in = sem("q_split"), sem("k_split"), sem("k_rest_in")
        v_ones = sem("v_ones")
        parts_in = [sem("parts_in0"), sem("parts_in1")]
        high_parts_in = [sem("high_parts_in0"), sem("high_parts_in1")]
        max_scores, max_read = sem("max_scores"), sem("max_read")
        max_turned, shift_split, shift_in = sem("max_turned"), sem("shift_split"), sem("shift_in")
        sums_log, sums_inverse = sem("sums_log"), sem("sums_inverse")
        shift_negated = sem("shift_negated")
        row_max_in, shift_chain = sem("row_max_in"), sem("shift_chain")
        st_ready, exp_done, pv_done = sem("st_ready"), sem("exp_done"), sem("pv_done")
        attn_read, sums_spread, attn_normed, attn_proj, x_updated = (
            sem("attn_read"), sem("sums_spread"), sem("attn_normed"), sem("attn_proj"),
            sem("x_updated"))

        GN, NQ, NK, NV, PROJ, M2, V2, AQ, AK, AV, M3, V3, FFN = range(13)
        reader = {GN: "dve", NQ: "act", NK: "dve", NV: "act", PROJ: "dve", M2: "dve", V2: "act", AQ: "act",
                  AK: "act", AV: "dve", M3: "dve", V3: "act", FFN: "dve"}
        count = {s: 2 if s == GN else NBLK for s in reader}
        ready_base = {s: sum(count[t] for t in range(s)) for s in reader}
        READY = sum(count.values())
        count[GN] = 1
        freed_base = {s: sum(count[t] for t in range(s) if reader[t] == reader[s]) for s in reader}
        FREED = {e: sum(count[t] for t in reader if reader[t] == e) for e in ("dve", "act")}
        freed = {"dve": freed_dve, "act": freed_act}

        def wait_parts(eng, b, g):
            eng.wait_ge(high_parts_in[g], (b + 1) * (16 * GH * len(HIGH_ROWS)))
            apart(eng)
            eng.wait_ge(parts_in[g], (b + 1) * (16 * GH * (2 * len(Q_PARTS) - len(HIGH_ROWS))))

        def wait_block(eng, b, stage, j):
            eng.wait_ge(block_ready, b * READY + (ready_base[stage] + j + 1))

        def wait_freed(eng, b, stage, j):
            eng.wait_ge(freed[reader[stage]], b * FREED[reader[stage]] + (freed_base[stage] + j + 1))

        def apart(eng):
            eng.sem_inc(paced, 1)

        def blk(t, j):
            return t[:, j * BLK:(j + 1) * BLK]

        def unit_index(b, unit):
            g, i, d = unit
            return b * AUNITS + (i + (g * NBLK + d))

        def columns(unit):
            g, i, d = unit
            start = i * BLK + d * BLK
            return slice(start, start + BLK) if isinstance(i, int) else bass.ds(start, BLK)

        def unit_queries(unit, h, at=0, n=BLK):
            g, i, d = unit
            start = i * (GH * BLK) + ((d * GH + h) * BLK + at)
            return slice(start, start + n) if isinstance(i, int) else bass.ds(start, n)

        def attention_units(eng, body):
            for g in range(GROUPS):
                def near(i, d):
                    k = g * NBLK + i + d
                    return (k // NBLK, k % NBLK, 0) if 0 <= k < AUNITS else None

                body({d: near(0, d) for d in (-1, 0, 1, 2)})
                with eng.Fori(1, NBLK - 2) as i:
                    body({d: (g, i, d) for d in (-1, 0, 1, 2)})
                for i in (NBLK - 2, NBLK - 1):
                    body({d: near(i, d) for d in (-1, 0, 1, 2)})

        def exp_buffer(c):
            return PB[2 if c == CHUNKS - 1 else c % 2]

        LAST_UNIT = (GROUPS - 1, NBLK - 1, 0)

        block = ctx.enter_context(nc.Block())

        @block.sync
        def _(sp):
            for s in (biased, turned_read, out_strip, pv_in, exp_done, attn_read, x_updated, pv_done):
                sp.sem_inc(s, PRIMED)
            for s in (shift_in, y_out):
                sp.sem_inc(s, 16 * PRIMED)
            def load(dst, src):
                sp.dma_start(dst, src).then_inc(weights_in, 16)

            xv = x.rearrange("b c y x -> b c (y x)")
            sp.dma_start(XF, xv[0]).then_inc(x_in, 16)
            load(C[:, :], consts)
            load(W_qkv[:, :], qkv_wT)
            load(W_proj[:, :], proj_wT)
            load(W_q[:, :], Wq)
            load(W_k[:, :], Wk)
            load(W_v[:, :], Wv)
            load(W_up, WT)
            load(codes, qidx)
            load(scale_blocks[:, :], scales.rearrange("(o n) -> o n", n=P // NF4_BLOCK))
            for n, v in enumerate((proj_b, bq, bk, bo)):
                load(bias_cols[:, n:n + 1], v.rearrange("(c o) -> c o", o=1))
            load(bv_rows[:, :], bass.AP(tensor=bv.tensor, offset=0, ap=[[0, P], [1, P]]))
            sp.wait_ge(setup_dve, 1)
            for g in range(GROUPS):
                for j in range(GH):
                    h = g * GH + j
                    load(W_o[32 * j:32 * j + ADIM, g, :], Wo[h * ADIM:(h + 1) * ADIM, :])
            stage1 = by_column.rearrange("p (t r k) -> p t r k", t=3, r=13)
            sp.wait_ge(table_filled, 3)
            for t, j0 in enumerate((0, QJ, SIDE - QJ)):
                for qi in range(QI):
                    for qj in range(QJ):
                        j = j0 + qj
                        at = first_key(j) - (j0 - PADJ)
                        rx = first_key(j) - j + KSZ - 1
                        q = qi * QJ + qj
                        sp.dma_start(stage1[q:P:QI * QJ, t, :, at:at + KSZ],
                                     rpb[:, :, rx:rx + KSZ]).then_inc(table_cols_in, 16)
            sp.wait_ge(table_cols_in, 16 * 3 * QI * QJ)
            for r, s in enumerate(ROW_TYPES):
                for q in range(QI * QJ):
                    i = QI * s + q // QJ
                    at = first_key(i) - window_row(s)
                    ry = first_key(i) - i + KSZ - 1
                    sp.dma_start(nat_bias[q:P:QI * QJ, r, :, at * WJ:(at + KSZ) * WJ],
                                 stage1[q:P:QI * QJ, :, ry:ry + KSZ, :].rearrange("p t r k -> p t (r k)")
                                 ).then_inc(table_rows_in, 16)
            zeros = zero_words[0:SIDE, :].rearrange("p (k e) -> p k e", k=PADJ)
            v_img = vT_dram.rearrange("(y x) c -> y x c", x=WIDE)
            sp.dma_start(v_img[:, 0:PADJ, :], zeros).then_inc(vpad_out, 16)
            sp.dma_start(v_img[:, PADJ + SIDE:WIDE, :], zeros).then_inc(vpad_out, 16)
            sp.wait_ge(vpad_out, 32)
            sp.wait_ge(table_rows_in, 16 * len(ROW_TYPES) * QI * QJ)

            yv = out.rearrange("b c y x -> b c (y x)")
            def load_values(row, k):
                for ky in range(WI):
                    src = bass.AP(tensor=vT_dram.tensor, offset=(row + ky) * (WIDE * P),
                                  ap=[[P, WJ], [QJ * P, UNITS], [1, P]])
                    sp.dma_start(VP[ky * WJ:(ky + 1) * WJ, k, :, :], src).then_inc(values_in[k], 16)

            with sp.Fori(0, images) as b:
                wait_freed(sp, b, NV, NBLK - 1)
                for r in range(2):
                    src = VTs[SIDE * r:SIDE * (r + 1), :, :]
                    dst = bass.AP(tensor=vT_dram.tensor, offset=(r * WIDE + PADJ) * P,
                                  ap=[[P, SIDE], [2 * WIDE * P, 28], [1, P]])
                    sp.dma_start(dst, src).then_inc(vT_out, 16)
                sp.wait_ge(vT_out, b * 32 + 32)
                sp.wait_ge(pads_zero, b * 3 + 3)

                load_values(window_row(0), 0)
                load_values(window_row(1), 1)
                with sp.Fori(1, STRIPS // 2 - 1) as t:
                    for k in range(2):
                        sp.wait_ge(pv_in, b * STRIPS + (t * 2 + (k - 1 + PRIMED)))
                        apart(sp)
                        load_values(t * 4 + (2 * k - 3), k)
                for k in range(2):
                    s = STRIPS - 2 + k
                    sp.wait_ge(pv_in, b * STRIPS + (s - 1 + PRIMED))
                    load_values(window_row(s), k)

                for g in range(GROUPS):
                    for part_q in range(3):
                        sp.wait_ge(q_split, b * 3 + (part_q + 1))
                        for h in range(GH):
                            c0 = (g * GH + h) * ADIM
                            for n in (n for n, m in enumerate(Q_PARTS) if m == part_q):
                                sp.dma_start(QP[n * ADIM:(n + 1) * ADIM, g, :].rearrange(
                                                 "p (i h t) -> p i h t", h=GH, t=BLK)[:, :, h, :],
                                             q_parts[c0:c0 + ADIM, part_q, :]).then_inc(parts_in[g], 16)
                    for part_k in (1, 2):
                        sp.wait_ge(k_split, b * 3 + (part_k + 1))
                        for h in range(GH):
                            c0 = (g * GH + h) * ADIM
                            for n in (n for n, m in enumerate(K_PARTS) if m == part_k):
                                sp.dma_start(KP[n * ADIM:(n + 1) * ADIM, g, h, :],
                                             k_parts[c0:c0 + ADIM, part_k, :]).then_inc(parts_in[g], 16)
                for g in range(GROUPS):
                    wait_parts(sp, b, g)
                apart(sp)
                sp.dma_start(XF, xv[bass.ds((b + 1) % images, 1)].rearrange("b c t -> (b c) t")).then_inc(x_in, 16)
                def send_shift(g, i):
                    unit = (g, i, 0)
                    for n in range(3):
                        sp.wait_ge(shift_split, unit_index(b, unit) * 3 + (n + 1))
                        sp.dma_start(QP[ROWS + n:ROWS + n + 1, g, unit_queries(unit, 0, n=GH * BLK)]
                                     .rearrange("p (o t) -> p o t", t=QN), shift_parts[:, n, :]
                                     ).then_inc(shift_in, 16)

                for g in range(GROUPS):
                    with sp.Fori(0, NBLK) as i:
                        send_shift(g, i)
                for j in range(NBLK):
                    wait_freed(sp, b, FFN, j)
                    sp.dma_start(yv[bass.ds(b, 1)].rearrange("b c t -> (b c) t")[:, j * BLK:(j + 1) * BLK],
                                 blk(X, j)).then_inc(y_out, 16)
            sp.wait_ge(y_out, images * (16 * NBLK) + 16 * PRIMED)
            sp.wait_ge(x_in, (images + 1) * 16)

        @block.gpsimd
        def _(pool):
            nc.gpsimd.memset(KP[96:128, :, :, :], 1.0).then_inc(setup_pool, 1)
            pool.wait_ge(setup_pool, 1)
            pool.wait_ge(weights_in, 16 * 22)

            with pool.Fori(0, images) as b:
                nc.gpsimd.memset(Kn, 0.0).then_inc(pads_zero, 1)
                pool.wait_ge(pads_zero, b * 3 + 1)
                apart(pool)
                nc.gpsimd.memset(PT[64:96, :, :, :], 0.0).then_inc(pads_zero, 1)
                nc.gpsimd.memset(VP[64:96, :, :, :], 0.0).then_inc(pads_zero, 1)
                pool.wait_ge(pads_zero, b * 3 + 3)
                apart(pool)

                def spread_queries(tok0, k):
                    for i in range(QI):
                        src = Qn[:, bass.ds(tok0 + i * SIDE, SIDE)] if not isinstance(tok0, int) else \
                            Qn[:, tok0 + i * SIDE:tok0 + (i + 1) * SIDE]
                        dst = QB[:, k, :, :].rearrange("p u (h i j) -> p u h i j", h=GH, i=QI)[:, :, :, i, :]
                        src = src.rearrange("p (u o j) -> p u o j", o=1, j=QJ).to_broadcast([P, UNITS, GH, QJ])
                        m = head_mask.rearrange("p (o h a) -> p o h a", o=1, a=1).to_broadcast([P, UNITS, GH, QJ])
                        nc.gpsimd.tensor_tensor(dst, src, m, ALU.mult).then_inc(queries_strip, 1)

                def subtract_max(n, k):
                    pool.wait_ge(biased, (n + 1) * 6 + PRIMED)
                    m = NM[:, k, 0:UNITS].rearrange("p (u o) -> p u o", o=1).to_broadcast([P, UNITS, KEYS])
                    nc.gpsimd.tensor_tensor(SC[:, k, :, :], SC[:, k, :, :], m, ALU.add).then_inc(shifted, 1)

                def normalise(n, k):
                    pool.wait_ge(summed, n * 2 + 2)
                    r = SUMS[:, 1, k, 0:UNITS].rearrange("p (u o) -> p u o", o=1).to_broadcast([P, UNITS, KEYS])
                    nc.gpsimd.tensor_tensor(SC[:, k, :, :], SC[:, k, :, :], r, ALU.mult).then_inc(normalised, 1)

                wait_freed(pool, b, NQ, NBLK - 1)
                apart(pool)
                base = b * STRIPS

                def queries(s, k):
                    if not (isinstance(s, int) and s < 2):
                        pool.wait_ge(scores_in, base + (s - 1))
                    spread_queries(s * (QI * SIDE), k)

                queries(0, 0)
                queries(1, 1)
                with pool.Fori(0, STRIPS // 2 - 1) as t:
                    for k in range(2):
                        subtract_max(base + (t * 2 + k), k)
                        queries(t * 2 + (k + 2), k)
                        normalise(base + (t * 2 + k), k)
                for k in range(2):
                    subtract_max(base + (STRIPS - 2 + k), k)
                    normalise(base + (STRIPS - 2 + k), k)

                pool.wait_ge(k_split, b * 3 + 1)
                apart(pool)
                for g in range(GROUPS):
                    for h in range(GH):
                        c0 = (g * GH + h) * ADIM
                        for n in HIGH_ROWS:
                            nc.gpsimd.dma_start(KP[n * ADIM:(n + 1) * ADIM, g, h, :],
                                                k_parts[c0:c0 + ADIM, 0, :]).then_inc(high_parts_in[g], 16)
                pool.wait_ge(q_split, b * 3 + 3)
                apart(pool)
                nc.gpsimd.memset(VA[:, 0:CHUNKS - 1, :, ADIM:32], 1.0).then_inc(v_ones, 1)
                nc.gpsimd.memset(VA[0:LAST, CHUNKS - 1, :, ADIM:32], 1.0).then_inc(v_ones, 1)
                pool.wait_ge(v_ones, b * 3 + 2)
                apart(pool)
                nc.gpsimd.memset(VA[LAST:P, CHUNKS - 1, :, :], 0.0).then_inc(v_ones, 1)
                pool.wait_ge(v_ones, b * 3 + 3)
                apart(pool)

                def split_shift(unit):
                    u = unit_index(b, unit)
                    pool.wait_ge(shift_negated, u + 1)
                    apart(pool)
                    nc.gpsimd.tensor_copy(shift_parts[:, 0, :], shift[:, 0, :]).then_inc(shift_split, 1)
                    pool.wait_ge(shift_split, u * 3 + 1)
                    nc.gpsimd.tensor_tensor(shift[:, 1, :], shift[:, 0, :], shift_parts[:, 0, :],
                                            ALU.subtract).then_inc(shift_chain, 1)
                    pool.wait_ge(shift_chain, u + 1)
                    apart(pool)
                    nc.gpsimd.tensor_copy(shift_parts[:, 1, :], shift[:, 1, :]).then_inc(shift_split, 1)
                    pool.wait_ge(shift_split, u * 3 + 2)
                    nc.gpsimd.tensor_tensor(shift_parts[:, 2, :], shift[:, 1, :], shift_parts[:, 1, :],
                                            ALU.subtract).then_inc(shift_split, 1)

                def normalise_unit(unit):
                    pool.wait_ge(sums_inverse, unit_index(b, unit) + 1)
                    nc.gpsimd.tensor_tensor(normed[:, :], tail[:, 0, :], tail[:, 1, :], ALU.mult).then_inc(attn_normed, 1)

                def attention_unit(units):
                    unit, after, before = units[0], units[1], units[-1]
                    if before is not None:
                        normalise_unit(before)
                    if after is not None:
                        split_shift(after)

                split_shift((0, 0, 0))
                attention_units(pool, attention_unit)
                normalise_unit(LAST_UNIT)
                wait_freed(pool, b, FFN, NBLK - 1)

        @block.tensor
        def _(pe):
            mm = nc.tensor.matmul

            pe.wait_ge(setup_dve, len(NF4) + 2)
            pe.wait_ge(weights_in, 16 * 22)
            pe.wait_ge(setup_pool, 1)
            mm(PS[:, 0, 0:P], normed[:, 0:P], W_up, start=True, stop=True).then_inc(setup_pe, 1)
            pe.wait_ge(setup_dve, len(NF4) + 3)

            with pe.Fori(0, images) as b:
                for n in range(2):
                    pe.wait_ge(gn_cols, b * 3 + (n + 1))
                    mm(PS[:, 7, n:n + 1], group_w, gn[:, 3 * n:3 * n + 1], start=True,
                       stop=True).then_inc(block_ready, 1)
                pe.wait_ge(gn_cols, b * 3 + 3)
                for j in range(NBLK):
                    mm(PS[:, j, 0:BLK], W_qkv[:, 0:P], blk(XN, j), start=True, stop=True).then_inc(block_ready, 1)
                for j in range(NBLK):
                    wait_freed(pe, b, NQ, j)
                    mm(PS[:, j, 0:BLK], W_qkv[:, P:2 * P], blk(XN, j), start=True, stop=True).then_inc(block_ready, 1)
                for j in range(NBLK):
                    wait_freed(pe, b, NK, j)
                    for c in range(4):
                        t0 = (4 * j + c) * VROW
                        m = mm(PS[0:VROW, j, c * P:(c + 1) * P], XN[:, t0:t0 + VROW], W_qkv[:, 2 * P:3 * P],
                               start=True, stop=True)
                    m.then_inc(block_ready, 1)
                wait_freed(pe, b, NV, NBLK - 1)
                pe.wait_ge(pads_zero, b * 3 + 3)

                base = b * STRIPS
                s_at = [(0, u) if u < 5 else (1, u - 5) if u < 10 else (2, u - 10) for u in range(UNITS)]

                def scores(n, k):
                    pe.wait_ge(keys_strip, n + 1)
                    pe.wait_ge(queries_strip, n * 2 + 2)
                    pe.wait_ge(biased, n * 6 + (PRIMED - 1))
                    apart(pe)
                    win = KS[:, k, :].rearrange("p (y x) -> p y x", x=WIDE)
                    for u in range(UNITS):
                        bk_, at = s_at[u]
                        for g in range(4):
                            r = slice(32 * g, 32 * g + 32)
                            m = mm(PS[r, bk_, at * KEYS:(at + 1) * KEYS], QB[r, k, u, :],
                                   win[r, :, u * QJ:u * QJ + WJ], start=True, stop=True,
                                   tile_position=(32 * g, 32 * g))
                    m.then_inc(scores_in, 1)

                def turn(n, k):
                    pe.wait_ge(normalised, n + 1)
                    for c in range(4):
                        pe.wait_ge(turned_read, n * 4 + (c - 3 + PRIMED))
                        for u in range(4 * c, min(4 * c + 4, UNITS)):
                            m = nc.tensor.transpose(PS[0:KEYS, TURN_BANKS[c], (u % 4) * P:(u % 4 + 1) * P],
                                                    SC[:, k, u, :], ident)
                        m.then_inc(turned, 1)

                def values(n, k, visit):
                    pe.wait_ge(turned_read, n * 4 + (4 + PRIMED))
                    pe.wait_ge(out_strip, n * 3 + PRIMED)
                    pe.wait_ge(values_in[k], visit)
                    for u in range(UNITS):
                        for g in range(4):
                            m = mm(PS[32 * g:32 * g + 32, 6, 32 * u:32 * u + 32],
                                   VP[0:KPAD, k, u, 32 * g:32 * g + 32], PT[0:KPAD, k, u, 32 * g:32 * g + 32],
                                   start=True, stop=True, tile_position=(0, 32 * g))
                    m.then_inc(pv_in, 1)

                VIS = 16 * WI
                per = STRIPS // 2 * VIS
                scores(base, 0)
                scores(base + 1, 1)
                turn(base, 0)
                with pe.Fori(1, STRIPS // 2) as t:
                    scores(base + t * 2, 0)
                    turn(base + (t * 2 - 1), 1)
                    values(base + (t * 2 - 2), 0, b * per + t * VIS)
                    scores(base + (t * 2 + 1), 1)
                    turn(base + t * 2, 0)
                    values(base + (t * 2 - 1), 1, b * per + t * VIS)
                values(base + (STRIPS - 2), 0, b * per + per)
                turn(base + (STRIPS - 1), 1)
                values(base + (STRIPS - 1), 1, b * per + per)
                pe.wait_ge(out_strip, b * (3 * STRIPS) + 3 * STRIPS + PRIMED)

                for j in range(NBLK):
                    mm(PS[:, j, 0:BLK], W_proj[:, :], blk(On, j), start=True, stop=True).then_inc(block_ready, 1)

                def layer_norm(mean_stage, var_stage, before, visit):
                    for j in range(NBLK):
                        wait_freed(pe, b, before, j) if before is not None else None
                        mm(PS[:, j, 0:BLK], mean_w, blk(X, j), start=True, stop=True).then_inc(block_ready, 1)
                    for j in range(NBLK):
                        wait_freed(pe, b, mean_stage, j)
                        pe.wait_ge(squared, b * (2 * NBLK) + (visit * NBLK + j + 1))
                        mm(PS[:, j, 0:BLK], mean_w, blk(SQ, j), start=True, stop=True).then_inc(block_ready, 1)

                layer_norm(M2, V2, PROJ, 0)
                for j in range(NBLK):
                    wait_freed(pe, b, V2, j)
                    pe.wait_ge(normed_in, b * (2 * NBLK) + (j + 1))
                    mm(PS[:, j, 0:BLK], W_q[:, :], blk(XN, j), start=True, stop=True).then_inc(block_ready, 1)
                for j in range(NBLK):
                    wait_freed(pe, b, AQ, j)
                    mm(PS[:, j, 0:BLK], W_k[:, :], blk(XN, j), start=True, stop=True).then_inc(block_ready, 1)
                for j in range(NBLK):
                    wait_freed(pe, b, AK, j)
                    for c in range(4 * j, min(4 * j + 4, CHUNKS)):
                        n = LAST if c == CHUNKS - 1 else P
                        m = mm(PS[0:n, j, (c % 4) * P:(c % 4 + 1) * P], XN[:, c * P:c * P + n], W_v[:, :],
                               start=True, stop=True)
                    m.then_inc(block_ready, 1)
                wait_freed(pe, b, AV, NBLK - 1)

                def score_for_max(unit, m):
                    q, h, j = max_step(m)
                    u = unit_index(b, unit)
                    bank, read = max_banks()[0][m]
                    if read is not None:
                        pe.wait_ge(max_read, u * MAXES + (read + 1))
                    elif bank != 7:
                        second = isinstance(unit[1], int) and unit == (0, 1, 0)
                        last = MAXES - 1 if second else max_banks()[1][bank]
                        pe.wait_ge(max_read, u * MAXES + (last + 1 - MAXES))
                    mm(PS[0:QN, bank, 0:BLK], QP[0:ROWS, unit[0], unit_queries(unit, h, q * QN, QN)],
                       KP[0:ROWS, unit[0], h, j * BLK:(j + 1) * BLK], start=True, stop=True).then_inc(max_scores, 1)

                def turn_maxima(unit):
                    pe.wait_ge(row_max_in, unit_index(b, unit) + 1)
                    apart(pe)
                    nc.tensor.transpose(PS[0:GH * QCH, 7, 0:QN], row_max[0:QN, :],
                                        ident[0:QN, 0:QN]).then_inc(max_turned, 1)

                def spread(unit):
                    pe.wait_ge(attn_read, unit_index(b, unit) + (1 + PRIMED))
                    pe.wait_ge(x_updated, unit_index(b, unit) + PRIMED)
                    mm(PS[:, 7, 0:BLK], pick_sum, tail[:, 0, :], start=True, stop=True).then_inc(sums_spread, 1)

                def project(unit):
                    pe.wait_ge(attn_normed, unit_index(b, unit) + 1)
                    mm(PS[:, 7, 0:BLK], W_o[:, unit[0], :], normed[:, :], start=True,
                       stop=True).then_inc(attn_proj, 1)

                def weigh(unit, c):
                    e = unit_index(b, unit)
                    pe.wait_ge(exp_done, e * (GH * CHUNKS) + (GH * c + GH + PRIMED))
                    if c == 0:
                        pe.wait_ge(attn_read, e + PRIMED)
                    for h in range(GH):
                        m = mm(PS[32 * h:32 * h + 32, 6, 0:BLK], VA[:, c, unit[0] * GH + h, :],
                               exp_buffer(c)[:, h, :], start=(c == 0), stop=(c == CHUNKS - 1),
                               tile_position=(0, 32 * h))
                    m.then_inc(pv_done, 1)

                def attention_unit(units):
                    unit, after, before = units[0], units[1], units[-1]
                    e = unit_index(b, unit)
                    g = unit[0]
                    weigh_at = 2 if after is not None else GH - 1

                    def scores_turned(c, h):
                        n = LAST if c == CHUNKS - 1 else P
                        at = c * GH + h
                        banks = ST_BANKS if after is not None else ALL_ST_BANKS
                        pe.wait_ge(exp_done, e * (GH * CHUNKS) + ((at + 1 - banks if at else 0) + PRIMED))
                        if n < P:
                            apart(pe)
                        mm(PS[0:n, at % banks, 0:BLK], KP[0:ROWSM, g, h, c * P:c * P + n],
                           QP[0:ROWSM, g, unit_queries(unit, h)], start=True, stop=True).then_inc(st_ready, 1)

                    for c in range(CHUNKS):
                        later = units[1 if c < MAX_CHUNKS else 2]
                        steps = list(max_steps(c)) if later is not None else []
                        if c == MAX_CHUNKS and later is not None and later[0] != g:
                            wait_parts(pe, b, later[0])
                        if c == TAIL_DONE and before is not None and after is not None:
                            pe.wait_ge(x_updated, e + PRIMED)
                            apart(pe)

                        def maxima(n):
                            for m in steps[:n]:
                                score_for_max(later, m)
                            del steps[:n]

                        maxima(1)
                        if c == 0:
                            pe.wait_ge(shift_in, (e + 1) * (16 * 3) + 16 * PRIMED)
                        for h in range(GH):
                            scores_turned(c, h)
                            if h == weigh_at and c > 0:
                                weigh(unit, c - 1)
                            if h == weigh_at and c == 0 and before is not None:
                                weigh(before, CHUNKS - 1)
                            maxima(1)
                        maxima(len(steps))
                        if c == SPREAD_AT and before is not None:
                            spread(before)
                        if c == PROJECT_AT and before is not None:
                            project(before)
                        if c == MAX_CHUNKS and after is not None:
                            turn_maxima(after)

                wait_parts(pe, b, 0)
                for m in range(0, MAXES, NBLK):
                    q, h, _ = max_step(m)
                    for j0, j1 in MAX_PIECES:
                        if m:
                            pe.wait_ge(max_read, b * (AUNITS * MAXES) + (m - NBLK + j1))
                        for j in range(j0, j1):
                            mm(PS[0:QN, j, 0:BLK], QP[0:ROWS, 0, unit_queries((0, 0, 0), h, q * QN, QN)],
                               KP[0:ROWS, 0, h, j * BLK:(j + 1) * BLK], start=True, stop=True).then_inc(max_scores, 1)
                for m in range(FIRST_STEPS):
                    score_for_max((0, 1, 0), m)
                turn_maxima((0, 0, 0))
                pe.wait_ge(v_ones, b * 3 + 3)
                attention_units(pe, attention_unit)
                weigh(LAST_UNIT, CHUNKS - 1)
                spread(LAST_UNIT)
                project(LAST_UNIT)
                pe.wait_ge(x_updated, b * AUNITS + (AUNITS + PRIMED))

                layer_norm(M3, V3, None, 1)
                for j in range(NBLK):
                    wait_freed(pe, b, V3, j)
                    pe.wait_ge(normed_in, b * (2 * NBLK) + (NBLK + j + 1))
                    mm(PS[:, j, 0:BLK], W_ffn[:, :], blk(XN, j), start=True, stop=True).then_inc(block_ready, 1)
                wait_freed(pe, b, FFN, NBLK - 1)

        @block.scalar
        def _(act):
            nc.scalar.preload_act_table_set("natural_log_exp_and_others")
            act.wait_ge(weights_in, 16 * 22)
            with act.Fori(0, images) as b:
                wait_block(act, b, GN, 1)
                nc.scalar.activation(gn[:, 7:8], PS[:, 7, 1:2], ACT.Ln, bias=eps5).then_inc(gn_log, 1)
                act.wait_ge(gn_log, b + 1)
                nc.scalar.activation(gn[:, 8:9], gn[:, 7:8], ACT.Exp, scale=-0.5).then_inc(gn_rstd, 1)
                for j in range(NBLK):
                    wait_block(act, b, NQ, j)
                    nc.scalar.activation(blk(Qn, j), PS[:, j, 0:BLK], ACT.Copy,
                                         scale=float(NDIM) ** -0.5).then_inc(freed_act, 1)
                for j in range(NBLK):
                    wait_block(act, b, NV, j)
                    nc.scalar.activation(VTs[0:VROW, 4 * j:4 * j + 4, :].rearrange("p c e -> p (c e)"),
                                         PS[0:VROW, j, :], ACT.Copy).then_inc(freed_act, 1)

                base = b * STRIPS
                wait_freed(act, b, NK, NBLK - 1)
                act.wait_ge(pads_zero, b * 3 + 3)

                def keys(n, row, k, first):
                    if not first:
                        act.wait_ge(scores_in, n - 1)
                    src = Kn[:, bass.ds(row * WIDE, WI * WIDE)] if not isinstance(row, int) else \
                        Kn[:, row * WIDE:(row + WI) * WIDE]
                    nc.scalar.activation(KS[:, k, :], src, ACT.Copy).then_inc(keys_strip, 1)

                def exponentials(n, k):
                    act.wait_ge(shifted, n + 1)
                    v = SC[:, k, :, :].rearrange("p u k -> p (u k)")
                    nc.scalar.activation(v, v, ACT.Exp).then_inc(exps, 1)

                def read_turned(n, k):
                    for c in range(4):
                        act.wait_ge(turned, n * 4 + (c + 1))
                        if c == 0:
                            act.wait_ge(pv_in, n + (PRIMED - 1))
                        u0, u1 = 4 * c, min(4 * c + 4, UNITS)
                        nc.scalar.activation(PT[0:KEYS, k, u0:u1, :].rearrange("p u e -> p (u e)"),
                                             PS[0:KEYS, TURN_BANKS[c], 0:(u1 - u0) * P], ACT.Copy).then_inc(turned_read, 1)

                keys(base, window_row(0), 0, True)
                keys(base + 1, window_row(1), 1, True)
                exponentials(base, 0)
                keys(base + 2, window_row(2), 0, False)
                with act.Fori(1, STRIPS // 2 - 2) as t:
                    read_turned(base + (t * 2 - 2), 0)
                    exponentials(base + (t * 2 - 1), 1)
                    keys(base + (t * 2 + 1), t * 4 - 1, 1, False)
                    read_turned(base + (t * 2 - 1), 1)
                    exponentials(base + t * 2, 0)
                    keys(base + (t * 2 + 2), t * 4 + 1, 0, False)
                for s in range(STRIPS - 5, STRIPS):
                    read_turned(base + (s - 1), (s - 1) % 2)
                    exponentials(base + s, s % 2)
                    if s + 2 < STRIPS:
                        keys(base + (s + 2), window_row(s + 2), s % 2, False)
                read_turned(base + (STRIPS - 1), 1)

                def layer_norm(mean_stage, var_stage):
                    for j in range(NBLK):
                        wait_freed(act, b, mean_stage, j)
                        nc.scalar.activation(blk(SQ, j), blk(XN, j), ACT.Square).then_inc(squared, 1)
                    for j in range(NBLK):
                        wait_block(act, b, var_stage, j)
                        nc.scalar.activation(blk(SD, j), PS[:, j, 0:BLK], ACT.Ln, bias=eps5).then_inc(freed_act, 1)
                        wait_freed(act, b, var_stage, j)
                        nc.scalar.activation(blk(SD, j), blk(SD, j), ACT.Exp, scale=-0.5).then_inc(rstd_in, 1)

                layer_norm(M2, V2)
                for stage, full, col in ((AQ, q_full, 1), (AK, k_full, 2)):
                    for j in range(NBLK):
                        wait_block(act, b, stage, j)
                        ins = nc.scalar.activation(blk(full, j), PS[:, j, 0:BLK], ACT.Identity,
                                                   bias=bias_cols[:, col:col + 1])
                        ins.then_inc(freed_act, 1)

                wait_freed(act, b, AK, NBLK - 1)
                nc.scalar.activation(k_parts[:, 0, :], k_full, ACT.Copy).then_inc(k_split, 1)
                act.wait_ge(k_rest_in, b + 1)
                nc.scalar.activation(k_parts[:, 1, :], k_rest, ACT.Copy).then_inc(k_split, 1)

                def negate_maxima(unit):
                    u = unit_index(b, unit)
                    act.wait_ge(max_turned, u + 1)
                    act.wait_ge(shift_in, u * (16 * 3) + 16 * PRIMED)
                    nc.scalar.activation(shift[:, 0, :], PS[0:GH * QCH, 7, 0:QN], ACT.Copy,
                                         scale=-1.0).then_inc(shift_negated, 1)

                def read_sums(unit):
                    u = unit_index(b, unit)
                    act.wait_ge(pv_done, u * CHUNKS + (CHUNKS + PRIMED))
                    act.wait_ge(x_updated, u + PRIMED)
                    nc.scalar.activation(tail[:, 0, :], PS[:, 6, 0:BLK], ACT.Copy).then_inc(attn_read, 1)

                def invert_sums(unit):
                    u = unit_index(b, unit)
                    act.wait_ge(sums_spread, u + 1)
                    nc.scalar.activation(tail[:, 1, :], PS[:, 7, 0:BLK], ACT.Ln).then_inc(sums_log, 1)
                    act.wait_ge(sums_log, u + 1)
                    nc.scalar.activation(tail[:, 1, :], tail[:, 1, :], ACT.Exp, scale=-1.0).then_inc(sums_inverse, 1)

                def attention_unit(units):
                    unit, after, before = units[0], units[1], units[-1]
                    e = unit_index(b, unit)
                    for c in range(CHUNKS):
                        n = LAST if c == CHUNKS - 1 else P
                        if c == INVERT_AT and before is not None:
                            invert_sums(before)
                        if c == MAX_CHUNKS + 1 and after is not None:
                            negate_maxima(after)
                        for h in range(GH):
                            at = c * GH + h
                            bank = at % (ST_BANKS if after is not None else ALL_ST_BANKS)
                            act.wait_ge(st_ready, e * (GH * CHUNKS) + (at + 1))
                            if h == 0:
                                act.wait_ge(pv_done, e * CHUNKS + ((c - 1 if c > 1 else c - 2) + PRIMED))
                            nc.scalar.activation(exp_buffer(c)[0:n, h, :], PS[0:n, bank, 0:BLK],
                                                 ACT.Exp, scale=float(ADIM) ** -0.5).then_inc(exp_done, 1)
                            if c == 0 and h == 1 and before is not None:
                                read_sums(before)

                negate_maxima((0, 0, 0))
                attention_units(act, attention_unit)
                read_sums(LAST_UNIT)
                invert_sums(LAST_UNIT)
                layer_norm(M3, V3)

        @block.vector
        def _(dve):
            V = nc.vector
            V.memset(W_o[:, :, :], 0.0).then_inc(setup_dve, 1)
            V.memset(nat_bias[:, :, :, :], MASKED).then_inc(table_filled, 1)
            V.memset(by_column, MASKED).then_inc(table_filled, 1)
            V.memset(zero_words, 0.0).then_inc(table_filled, 1)
            dve.wait_ge(weights_in, 16 * 22)
            w, term = normed[:, 0:P], tail[:, 0, 0:P]
            for k, value in enumerate(NF4):
                V.tensor_scalar(term, codes, float(k), value, ALU.is_equal, ALU.mult).then_inc(dve_chain, 1)
                dve.wait_ge(dve_chain, k + 1)
                if k == 0:
                    V.tensor_copy(w, term).then_inc(setup_dve, 1)
                else:
                    V.tensor_tensor(w, w, term, ALU.add).then_inc(setup_dve, 1)
                dve.wait_ge(setup_dve, k + 2)
            wv = w.rearrange("p (n e) -> p n e", e=NF4_BLOCK)
            s = scale_blocks[:, :].rearrange("p (n o) -> p n o", o=1).to_broadcast([P, P // NF4_BLOCK, NF4_BLOCK])
            V.tensor_tensor(wv, wv, s, ALU.mult).then_inc(setup_dve, 1)
            dve.wait_ge(setup_pe, 1)
            V.tensor_copy(W_ffn[:, :], PS[:, 0, 0:P]).then_inc(setup_dve, 1)

            def image_stats(k):
                dve.wait_ge(x_in, k * 16 + 16)
                for j in range(NBLK):
                    V.bn_stats(stats[:, j, :], blk(XF, j)).then_inc(stats_in, 1)

            image_stats(0)
            with dve.Fori(0, images) as b:
                chain = [0]

                def own(ins):
                    ins.then_inc(dve_chain, 1)
                    chain[0] += 1
                    dve.wait_ge(dve_chain, b * OWN + (len(NF4) + chain[0]))

                dve.wait_ge(stats_in, (b + 1) * NBLK)
                apart(dve)
                V.bn_aggr(gn[:, 0:2], stats[:, :, :]).then_inc(gn_cols, 1)
                wait_block(dve, b, GN, 0)
                V.tensor_copy(gn[:, 4:5], PS[:, 7, 0:1]).then_inc(freed_dve, 1)
                wait_freed(dve, b, GN, 0)
                own(V.tensor_tensor(gn[:, 5:6], gn[:, 0:1], gn[:, 4:5], ALU.subtract))
                own(V.tensor_tensor(gn[:, 6:7], gn[:, 5:6], gn[:, 5:6], ALU.mult))
                V.tensor_tensor(gn[:, 3:4], gn[:, 6:7], gn[:, 1:2], ALU.add).then_inc(gn_cols, 1)
                dve.wait_ge(gn_rstd, b + 1)
                V.tensor_scalar(XN, XF, gn[:, 4:5], gn[:, 8:9], ALU.subtract, ALU.mult).then_inc(gn_cols, 1)
                dve.wait_ge(pads_zero, b * 3 + 3)
                k_img = Kn.rearrange("p (y x) -> p y x", x=WIDE)
                rows = BLK // SIDE
                for j in range(NBLK):
                    wait_block(dve, b, NK, j)
                    V.tensor_copy(k_img[:, rows * j:rows * (j + 1), PADJ:PADJ + SIDE],
                                  PS[:, j, 0:BLK].rearrange("p (y x) -> p y x", x=SIDE)).then_inc(freed_dve, 1)

                base = b * STRIPS
                dve.wait_ge(table_rows_in, 16 * len(ROW_TYPES) * QI * QJ)
                dve.wait_ge(vpad_out, 32)

                def add_bias(n, k, row_type, first):
                    dve.wait_ge(scores_in, n + 1)
                    if not first:
                        dve.wait_ge(turned, (n - 1) * 4)
                    for bk_, u0, u1, kind in ((0, 0, 1, 0), (0, 1, 5, 1), (1, 5, 10, 1), (2, 10, 13, 1), (2, 13, 14, 2)):
                        at = (u0 - (0, 5, 10)[bk_]) * KEYS
                        m = u1 - u0
                        V.tensor_tensor(
                            SC[:, k, u0:u1, :], PS[:, bk_, at:at + m * KEYS].rearrange("p (u k) -> p u k", u=m),
                            nat_bias[:, row_type, kind:kind + 1, :].to_broadcast([P, m, KEYS]),
                            ALU.add).then_inc(biased, 1)
                    dve.wait_ge(biased, n * 6 + 5 + PRIMED)
                    V.tensor_reduce(NM[:, k, 0:UNITS], SC[:, k, :, :], AX.X, ALU.max, negate=True).then_inc(biased, 1)

                def sum_up(n, k):
                    dve.wait_ge(exps, n + 1)
                    V.tensor_reduce(SUMS[:, 0, k, 0:UNITS], SC[:, k, :, :], AX.X, ALU.add).then_inc(summed, 1)
                    dve.wait_ge(summed, n * 2 + 1)
                    V.reciprocal(SUMS[:, 1, k, 0:UNITS], SUMS[:, 0, k, 0:UNITS]).then_inc(summed, 1)

                def finish(n, k, tok0):
                    dve.wait_ge(pv_in, n + (1 + PRIMED))
                    V.tensor_tensor(PVM.rearrange("p (u h q) -> p u h q", u=UNITS, h=GH),
                                    PS[:, 6, 0:BLK].rearrange("p (u h q) -> p u h q", u=UNITS, h=GH),
                                    head_mask.rearrange("p (o h a) -> p o h a", o=1, a=1)
                                    .to_broadcast([P, UNITS, GH, QI * QJ]), ALU.mult).then_inc(out_strip, 1)
                    dve.wait_ge(out_strip, n * 3 + (1 + PRIMED))
                    v = PVM.rearrange("p (u h i j) -> p i u j h", u=UNITS, h=GH, i=QI)
                    for i in range(QI):
                        o = On[:, tok0 + i * SIDE:tok0 + (i + 1) * SIDE] if isinstance(tok0, int) else \
                            On[:, bass.ds(tok0 + i * SIDE, SIDE)]
                        V.tensor_reduce(o.rearrange("p (u j) -> p u j", u=UNITS), v[:, i], AX.X,
                                        ALU.add).then_inc(out_strip, 1)

                ROW = QI * SIDE
                add_bias(base, 0, 0, True)
                sum_up(base, 0)
                add_bias(base + 1, 1, 1, True)
                sum_up(base + 1, 1)
                with dve.Fori(1, STRIPS // 2 - 1) as t:
                    for k in range(2):
                        add_bias(base + (t * 2 + k), k, 2, False)
                        finish(base + (t * 2 + (k - 2)), k, t * (2 * ROW) + (k - 2) * ROW)
                        sum_up(base + (t * 2 + k), k)
                for s in (STRIPS - 2, STRIPS - 1):
                    add_bias(base + s, s % 2, s - (STRIPS - 5), False)
                    finish(base + (s - 2), s % 2, (s - 2) * ROW)
                    sum_up(base + s, s % 2)
                finish(base + (STRIPS - 2), 0, (STRIPS - 2) * ROW)
                finish(base + (STRIPS - 1), 1, (STRIPS - 1) * ROW)

                dve.wait_ge(y_out, b * (16 * NBLK) + 16 * PRIMED)
                for j in range(NBLK):
                    wait_block(dve, b, PROJ, j)
                    V.scalar_tensor_tensor(out=blk(X, j), in0=PS[:, j, 0:BLK], scalar=bias_cols[:, 0:1],
                                           in1=blk(XF, j), op0=ALU.add, op1=ALU.add).then_inc(freed_dve, 1)

                def layer_norm(mean_stage, var_stage, visit):
                    for j in range(NBLK):
                        wait_block(dve, b, mean_stage, j)
                        V.tensor_tensor(blk(XN, j), blk(X, j), PS[:, j, 0:BLK], ALU.subtract).then_inc(freed_dve, 1)
                    for j in range(NBLK):
                        dve.wait_ge(rstd_in, b * (2 * NBLK) + (visit * NBLK + j + 1))
                        V.tensor_tensor(blk(XN, j), blk(XN, j), blk(SD, j), ALU.mult).then_inc(normed_in, 1)

                layer_norm(M2, V2, 0)
                wait_freed(dve, b, AQ, NBLK - 1)
                def split_step(ins, n):
                    ins.then_inc(q_split, 1)
                    dve.wait_ge(q_split, b * 3 + n)

                split_step(V.tensor_copy(q_parts[:, 0, :], q_full), 1)
                own(V.tensor_tensor(q_rest, q_full, q_parts[:, 0, :], ALU.subtract))
                split_step(V.tensor_copy(q_parts[:, 1, :], q_rest), 2)
                V.tensor_tensor(q_parts[:, 2, :], q_rest, q_parts[:, 1, :], ALU.subtract).then_inc(q_split, 1)
                dve.wait_ge(k_split, b * 3 + 1)
                V.tensor_tensor(k_rest, k_full, k_parts[:, 0, :], ALU.subtract).then_inc(k_rest_in, 1)
                dve.wait_ge(k_split, b * 3 + 2)
                V.tensor_tensor(k_parts[:, 2, :], k_rest, k_parts[:, 1, :], ALU.subtract).then_inc(k_split, 1)
                for j in range(NBLK):
                    wait_block(dve, b, AV, j)
                    m = min(4, CHUNKS - 4 * j)
                    n = LAST if m == 1 else P
                    V.tensor_tensor(VA[0:n, 4 * j:4 * j + m, :, 0:ADIM],
                                    PS[0:n, j, 0:m * P].rearrange("p (c h e) -> p c h e", c=m, h=AHEADS),
                                    bv_rows[0:n, :].rearrange("p (o h e) -> p o h e", o=1, h=AHEADS)
                                    .to_broadcast([n, m, AHEADS, ADIM]), ALU.add).then_inc(freed_dve, 1)

                def take_max(unit, m):
                    q, h, j = max_step(m)
                    dve.wait_ge(max_scores, unit_index(b, unit) * MAXES + (m + 1))
                    V.tensor_reduce(block_max[0:QN, h * QCH + q, j:j + 1], PS[0:QN, max_banks()[0][m][0], 0:BLK],
                                    AX.X, ALU.max).then_inc(max_read, 1)

                def row_maxima(unit):
                    dve.wait_ge(max_read, (unit_index(b, unit) + 1) * MAXES)
                    V.tensor_reduce(row_max[0:QN, :], block_max[0:QN, :, :], AX.X, ALU.max).then_inc(row_max_in, 1)
                    dve.wait_ge(row_max_in, unit_index(b, unit) + 1)

                def update_x(unit):
                    dve.wait_ge(attn_proj, unit_index(b, unit) + 1)
                    xb = X[:, columns(unit)]
                    if unit[0] == 0:
                        ins = V.scalar_tensor_tensor(out=xb, in0=PS[:, 7, 0:BLK], scalar=bias_cols[:, 3:4],
                                                     in1=xb, op0=ALU.add, op1=ALU.add)
                    else:
                        ins = V.tensor_tensor(xb, xb, PS[:, 7, 0:BLK], ALU.add)
                    ins.then_inc(x_updated, 1)

                def attention_unit(units):
                    unit, after, before = units[0], units[1], units[-1]
                    for c in range(CHUNKS):
                        if before is not None and c == UPDATE_AT:
                            update_x(before)
                        if c == MAX_CHUNKS and after is not None:
                            row_maxima(after)
                        later = units[1 if c < MAX_CHUNKS else 2]
                        for m in max_steps(c) if later is not None else ():
                            take_max(later, m)

                for m in range(0, MAXES, NBLK):
                    q, h, _ = max_step(m)
                    for j0, j1 in MAX_PIECES:
                        dve.wait_ge(max_scores, b * (AUNITS * MAXES) + (m + j1))
                        V.tensor_reduce(block_max[0:QN, h * QCH + q, j0:j1], PS[0:QN, j0:j1, 0:BLK],
                                        AX.X, ALU.max).then_inc(max_read, j1 - j0)
                row_maxima((0, 0, 0))
                for m in range(FIRST_STEPS):
                    take_max((0, 1, 0), m)
                attention_units(dve, attention_unit)
                image_stats(b + 1)
                update_x(LAST_UNIT)
                dve.wait_ge(x_updated, b * AUNITS + (AUNITS + PRIMED))

                layer_norm(M3, V3, 1)
                for j in range(NBLK):
                    wait_block(dve, b, FFN, j)
                    V.tensor_tensor(blk(X, j), blk(X, j), PS[:, j, 0:BLK], ALU.add).then_inc(freed_dve, 1)
                assert chain[0] == OWN, chain


def kernel(x, L0_conv_qkv_w, L0_conv_rpb, L0_conv_proj_w, L0_conv_proj_b, L1_attn_Wq, L1_attn_bq, L1_attn_Wk,
           L1_attn_bk, L1_attn_Wv, L1_attn_bv, L1_attn_Wo, L1_attn_bo, L1_ffn_qidx, L1_ffn_scales, L1_ffn_W):
    import concourse.bacc as bacc
    from concourse.bass_utils import run_bass_kernel_spmd

    args = {
        "x": x, "consts": shape_constants(), "qkv_wT": np.asarray(L0_conv_qkv_w).T, "rpb": L0_conv_rpb,
        "proj_wT": np.asarray(L0_conv_proj_w).T, "proj_b": L0_conv_proj_b, "Wq": L1_attn_Wq, "bq": L1_attn_bq,
        "Wk": L1_attn_Wk, "bk": L1_attn_bk, "Wv": L1_attn_Wv, "bv": L1_attn_bv, "Wo": L1_attn_Wo,
        "bo": L1_attn_bo, "qidx": L1_ffn_qidx, "scales": L1_ffn_scales, "WT": np.asarray(L1_ffn_W).T,
    }
    nc = bacc.Bacc("TRN2", target_bir_lowering=False, num_devices=1)
    arrays, aps = {}, {}
    for name, a in args.items():
        a = np.ascontiguousarray(a)
        arrays[f"in_{name}"] = a
        aps[name] = nc.dram_tensor(f"in_{name}", a.shape, mybir.dt.from_np(a.dtype), kind="ExternalInput").ap()
    aps["out"] = nc.dram_tensor("out_y", arrays["in_x"].shape, F32, kind="ExternalOutput").ap()
    hybrid_block(nc, arrays["in_x"].shape[0], **aps)
    r = run_bass_kernel_spmd(nc, [arrays], core_ids=[0])
    return r.results[0]["out_y"]
```
